# Optimizing a Trainium2 kernel written in Bass

```python
import numpy as np
import jax
import jax.numpy as jnp

def _softmax(x, axis=-1):
    return jax.nn.softmax(x, axis=axis)

def _gelu(x):
    return jax.nn.gelu(x, approximate=True)

def _silu(x):
    return jax.nn.silu(x)

def _sigmoid(x):
    return jax.nn.sigmoid(x)

def _layernorm(x, axis=-1, eps=1e-05):
    m = jnp.mean(x, axis=axis, keepdims=True)
    v = jnp.var(x, axis=axis, keepdims=True)
    return (x - m) / jnp.sqrt(v + eps)

def _scatter_add(tgt, idx, src, axis=0):
    return tgt.at[idx].add(src)

def _segment_sum(src, seg, n):
    return jax.ops.segment_sum(src, seg, n)
kernel_name = 'mk_sandwich_d1_jaxref_r8_b4273a'

def setup_inputs(seed: int=0):
    np.random.seed(seed)
    _w = jnp.asarray

    def _L0_attn_setup():
        import jax, jax.numpy as jnp
        import numpy as np
        B, S, D = (2, 256, 128)
        H = 16
        HD = D // H
        THETA = 1000.0
        SCALE = 0.02

        def _rope(t, cos, sin):
            even = t[..., ::2]
            odd = t[..., 1::2]
            return jnp.concatenate([even * cos - odd * sin, odd * cos + even * sin], axis=-1)
        key = jax.random.key(seed)
        k0, k1, k2, k3, k4 = jax.random.split(key, 5)
        x = jax.random.normal(k0, (B, S, D), dtype=jnp.float32)
        wq = SCALE * jax.random.normal(k1, (D, D), dtype=jnp.float32)
        wk = SCALE * jax.random.normal(k2, (D, HD), dtype=jnp.float32)
        wv = SCALE * jax.random.normal(k3, (D, HD), dtype=jnp.float32)
        wo = SCALE * jax.random.normal(k4, (D, D), dtype=jnp.float32)
        return {'x': x, 'wq': wq, 'wk': wk, 'wv': wv, 'wo': wo}
    _L0_attn_in = _L0_attn_setup()

    def _L0_ffn_setup():
        import jax, jax.numpy as jnp
        import numpy as np
        DIM = 128

        def _reference_tuple_inner(x, W_r, W_k, W_v, mu_r, mu_k):
            B, T, C = x.shape
            x_prev = jnp.concatenate([jnp.zeros((B, 1, C), x.dtype), x[:, :-1, :]], axis=1)
            xr = mu_r * x + (1.0 - mu_r) * x_prev
            xk = mu_k * x + (1.0 - mu_k) * x_prev
            r = jax.nn.sigmoid(jnp.einsum('btc,dc->btd', xr, W_r))
            k = jnp.einsum('btc,dc->btd', xk, W_k)
            k_act = jnp.square(jax.nn.relu(k))
            out = r * jnp.einsum('btc,dc->btd', k_act, W_v)
            new_state = x[:, -1, :]
            return (out, new_state)
        key = jax.random.key(seed)
        ks = jax.random.split(key, 6)
        B, T, C = (8, 256, DIM)
        x = jax.random.normal(ks[0], (B, T, C), dtype=jnp.float32)
        s = 1.0 / np.sqrt(C)
        W_r = jax.random.uniform(ks[1], (C, C), jnp.float32, -s, s)
        W_k = jax.random.uniform(ks[2], (C, C), jnp.float32, -s, s)
        W_v = jax.random.uniform(ks[3], (C, C), jnp.float32, -s, s)
        mu_r = jax.random.uniform(ks[4], (C,), jnp.float32)
        mu_k = jax.random.uniform(ks[5], (C,), jnp.float32)
        return {'x': x, 'W_r': W_r, 'W_k': W_k, 'W_v': W_v, 'mu_r': mu_r, 'mu_k': mu_k}
    _L0_ffn_in = _L0_ffn_setup()
    _d = {'L0_attn_x': _L0_attn_in['x'], 'L0_attn_wq': _L0_attn_in['wq'], 'L0_attn_wk': _L0_attn_in['wk'], 'L0_attn_wv': _L0_attn_in['wv'], 'L0_attn_wo': _L0_attn_in['wo'], 'L0_ffn_W_r': _L0_ffn_in['W_r'], 'L0_ffn_W_k': _L0_ffn_in['W_k'], 'L0_ffn_W_v': _L0_ffn_in['W_v'], 'L0_ffn_mu_r': _L0_ffn_in['mu_r'], 'L0_ffn_mu_k': _L0_ffn_in['mu_k']}
    _x0 = _d['L0_attn_x']
    _d['L0_attn_x'] = jax.random.normal(jax.random.fold_in(jax.random.key(seed), 1), (4, 1024, 128), dtype=_x0.dtype)
    del _x0
    return _d

def reference(L0_attn_x, L0_attn_wq, L0_attn_wk, L0_attn_wv, L0_attn_wo, L0_ffn_W_r, L0_ffn_W_k, L0_ffn_W_v, L0_ffn_mu_r, L0_ffn_mu_k):

    def _L0_attn_ref(x, wq, wk, wv, wo):
        import jax, jax.numpy as jnp
        import numpy as np
        B, S, D = (2, 256, 128)
        H = 16
        HD = D // H
        THETA = 1000.0
        SCALE = 0.02

        def _rope(t, cos, sin):
            even = t[..., ::2]
            odd = t[..., 1::2]
            return jnp.concatenate([even * cos - odd * sin, odd * cos + even * sin], axis=-1)
        b, s, d = x.shape
        freqs = 1.0 / THETA ** (jnp.arange(0, HD, 2, dtype=jnp.float32) / HD)
        ang = jnp.arange(s, dtype=jnp.float32)[:, None] * freqs[None, :]
        cos, sin = (jnp.cos(ang), jnp.sin(ang))
        q = (x @ wq.T).reshape(b, s, H, HD).transpose(0, 2, 1, 3)
        k = x @ wk
        v = x @ wv
        q = _rope(q, cos[None, None], sin[None, None])
        k = _rope(k, cos[None], sin[None])
        scores = jnp.einsum('bhqd,bkd->bhqk', q, k) / np.float32(np.sqrt(HD))
        causal = jnp.triu(jnp.ones((s, s), dtype=bool), 1)
        scores = jnp.where(causal[None, None], -jnp.inf, scores)
        w = jax.nn.softmax(scores, axis=-1)
        out = jnp.einsum('bhqk,bkd->bhqd', w, v)
        out = out.transpose(0, 2, 1, 3).reshape(b, s, d)
        return out @ wo.T

    def _L0_ffn_ref(x, W_r, W_k, W_v, mu_r, mu_k):
        import jax, jax.numpy as jnp
        import numpy as np
        DIM = 128

        def _reference_tuple_inner(x, W_r, W_k, W_v, mu_r, mu_k):
            B, T, C = x.shape
            x_prev = jnp.concatenate([jnp.zeros((B, 1, C), x.dtype), x[:, :-1, :]], axis=1)
            xr = mu_r * x + (1.0 - mu_r) * x_prev
            xk = mu_k * x + (1.0 - mu_k) * x_prev
            r = jax.nn.sigmoid(jnp.einsum('btc,dc->btd', xr, W_r))
            k = jnp.einsum('btc,dc->btd', xk, W_k)
            k_act = jnp.square(jax.nn.relu(k))
            out = r * jnp.einsum('btc,dc->btd', k_act, W_v)
            new_state = x[:, -1, :]
            return (out, new_state)
        return _reference_tuple_inner(x, W_r, W_k, W_v, mu_r, mu_k)[0]
    x = L0_attn_x
    x = x + _layernorm(_L0_attn_ref(_layernorm(x, axis=-1), L0_attn_wq, L0_attn_wk, L0_attn_wv, L0_attn_wo), axis=-1)
    x = x + _layernorm(_L0_ffn_ref(_layernorm(x, axis=-1), L0_ffn_W_r, L0_ffn_W_k, L0_ffn_W_v, L0_ffn_mu_r, L0_ffn_mu_k), axis=-1)
    return x

_drawn_inputs = setup_inputs


def setup_inputs(seed=0):
    import zlib

    import numpy as np

    out = dict(_drawn_inputs(seed))
    spreads = {}
    factors = {}
    for name, (base, spread) in spreads.items():
        noise = np.random.default_rng([zlib.crc32(name.encode()), seed]).standard_normal(out[name].shape)
        drawn = base * np.exp(spread * noise) if base else spread * noise
        out[name] = jnp.asarray(drawn.astype(out[name].dtype))
    for name, factor in factors.items():
        out[name] = (out[name] * factor).astype(out[name].dtype)
    return out
```

```python
from contextlib import ExitStack

import numpy as np

import concourse.bass as bass
from concourse import mybir

F32 = mybir.dt.float32
BF16 = mybir.dt.bfloat16
ALU = mybir.AluOpType
ACT = mybir.ActivationFunctionType
AX_X = mybir.AxisListType.X

P = 128
B, S, D = 4, 1024, 128
H, HD = 16, 8
THETA = 1000.0
EPS = 1e-5
NT = S // P
HALF = S // 2
G = 4
SCALE = 1.0 / float(np.sqrt(HD))
NEG = -1e30
LOWEST = -3e38
Q_PART = (0, 0, 0, 1, 1, 2)
K_PART = (0, 1, 2, 0, 1, 0)
KROWS = 8 * len(Q_PART)
ROWS = KROWS + 3
VW = 32
P_RING = 8
AHEAD = 16
LAG = 3
EVAC_LAG = 2

W_QA, W_QB, W_KA, W_KB, W_V = 0, 128, 256, 288, 320
W_O, W_R, W_K, W_VF, W_MU = 328, 456, 584, 712, 840
W_COLS = 842
C_ID, C_MASK, C_KCOS, C_KSIN, C_COS, C_SIN = 0, 128, 640, 1152, 1664, 2688
C_COLS = 3712



def main_units():
    out = []
    for qh in range(2):
        for kt in range(4 * (qh + 1)):
            width = HALF - P * max(0, kt - 4 * qh)
            pairs = [(0,), (1,)] if width > 256 else [(0, 1)]
            out += [(qh, kt, rs, width) for rs in pairs]
    return out


UNITS = main_units()


def max_jobs():
    out = []
    for t in range(NT):
        if t >= 4:
            out += [(a, (r,), t, 0, HALF) for r in range(2) for a in range(2)]
        k0 = HALF * (t // 4)
        n = (t + 1) * P - k0
        for rs in ([(0, 1)] if n <= 256 else [(0,), (1,)]):
            out += [(a, rs, t, k0, n) for a in range(2)]
    return out


MAX_JOBS = max_jobs()

ACT_JOBS = ("xT", "mT", "y", "nT", "r", "k")
DVE_JOBS = ("max", "qa", "qb", "ka", "kb", "v", "f")


def pre_items(b):
    return ([("x_load", b), ("x_stats", b), ("x_norm", b), ("xT", b, 0), ("xT", b, 1)]
            + [("ka", b), ("kb", b), ("k_split", b, 0), ("k_split", b, 1), ("k_split", b, 2),
               ("k_split", b, 3), ("k_split", b, 4), ("k_store", b), ("kA_load", b)]
            + [("qa", b, 0), ("qb", b, 0)] + [("q_split", b, 0, i) for i in range(5)]
            + [("qa", b, 1), ("qb", b, 1)] + [("q_split", b, 1, i) for i in range(5)]
            + [("q_store", b), ("q_load", b, 0), ("q_load", b, 1), ("v", b, 0), ("v", b, 1)])


def post_items(b, h):
    return [("o_norm", b, h), ("y", b, h), ("y_stats", b, h), ("y_norm", b, h), ("x1", b, h),
            ("x1_stats", b, h), ("x1_norm", b, h), ("nT", b, h), ("diff", b, h), ("mix", b, h),
            ("r", b, h), ("k", b, h), ("sq", b, h), ("sig", b, h), ("f", b, h), ("f_stats", b, h),
            ("f_norm", b, h), ("out", b, h)]


COST = {"max": 0.6, "y_stats": 1.1, "x1_stats": 1.1, "f_stats": 1.1, "x_stats": 2.2, "x_norm": 1.1,
        "y_norm": .55, "x1_norm": .55, "f_norm": .55, "o_norm": 1.2, "mix": 1.2, "sig": 1., "f": .6,
        "qa": .6, "qb": .6, "ka": .6, "kb": .6}


def weave(jobs, items, every, start=0):
    out, items = [], list(items)
    for i, job in enumerate(jobs):
        out.append(job)
        if i >= start and (i - start) % every == every - 1 and items:
            out.append(items.pop(0))
    return out + items


def timeline():
    def maxima(b, g):
        return [("max", b, g, i) for i in range(len(MAX_JOBS))]

    def closing(b, g):
        return [("m_max", b, g)] + [("m_split", b, g, i) for i in range(5)] + [("mT", b, g), ("m_load", b, g)]

    head = pre_items(0) + maxima(0, 0)
    early = weave(maxima(0, 1), [("q_load", 0, 2), ("q_load", 0, 3), ("kB_load", 0), ("vB_copy", 0)], 1)
    head += weave(early[:AHEAD], closing(0, 0), 1)
    early = early[AHEAD:] + weave(maxima(0, 2)[:AHEAD], closing(0, 1), 1)
    early2 = maxima(0, 2)[AHEAD:] + weave(maxima(0, 3)[:AHEAD], closing(0, 2), 1)

    def steady(b):
        s = weave(maxima(b, 3)[AHEAD:], pre_items(b + 1), 1)
        s += weave(maxima(b + 1, 0), closing(b, 3), 1)
        s += weave(maxima(b + 1, 1), closing(b + 1, 0), 1)
        s += weave(maxima(b + 1, 2), closing(b + 1, 1) + post_items(b, 0) + post_items(b, 1), 1)
        return s + weave(maxima(b + 1, 3)[:AHEAD], closing(b + 1, 2), 1)

    def freed_by(u):
        _, b, g, i = u
        out = []
        if i == len(UNITS) - 1 and g >= 2 and b + 1 < B:
            out.append(("q_load", b + 1, g))
        if i == len(UNITS) - 1 and g == 3:
            out += [("kB_load", b + 1)] * (b + 1 < B) + [("xres_load", b)]
        if i == LAG + EVAC_LAG + 1 and g == 0 and b > 0:
            out.append(("vB_copy", b))
        return out

    def with_main(units, side):
        total = sum(COST.get(i[0], 0.05) for i in side)
        out, spent, at = [], 0.0, 0
        for n, u in enumerate(units):
            while at < len(side) and spent < total * n / len(units):
                out.append(side[at])
                spent += COST.get(side[at][0], 0.05)
                at += 1
            out.append(u)
            out += freed_by(u)
        return out + side[at:]

    def units(b, g):
        return [("unit", b, g, i) for i in range(len(UNITS))]

    def stretch(b, last=False):
        if not last:
            return with_main(units(b, 2) + units(b, 3) + units(b + 1, 0) + units(b + 1, 1), steady(b))
        s = maxima(b, 3)[AHEAD:] + closing(b, 3)
        return with_main(units(b, 2), s) + with_main(units(b, 3), [])

    start = head + with_main(units(0, 0), early) + with_main(units(0, 1), early2)
    raw = start + [("loop",)]
    for b in range(B - 1):
        raw += stretch(b) + [("loop",)]
    raw += stretch(B - 1, True)
    out, pending, n = [], [], 0
    for e in raw:
        out.append(e)
        if e[0] != "unit":
            continue
        n += 1
        _, b, g, i = e
        qh, kt, _, _ = UNITS[i]
        if i + 1 == len(UNITS) or UNITS[i + 1][:2] != (qh, kt):
            pending.append((n + LAG, ("pv", b, g, qh, kt)))
            if kt == 4 * qh + 3:
                pending.append((n + LAG + EVAC_LAG, ("o_copy", b, g, qh)))
        while pending and min(pending)[0] <= n:
            nxt = min(pending)
            pending.remove(nxt)
            out.append(nxt[1])
    for nxt in sorted(pending):
        out.append(nxt[1])
    p0, p1 = post_items(B - 1, 0), post_items(B - 1, 1)
    out += p0 + p1
    cuts = [i for i, e in enumerate(out) if e == ("loop",)]
    at = {e: n for n, e in enumerate(out)}
    for b in range(B):
        for g in range(G):
            assert at["m_load", b, g] < at["unit", b, g, 0], (b, g)
        for h in range(2):
            assert at["o_copy", b, 3, h] < at["o_norm", b, h], (b, h)
        assert at["xres_load", b] < at["x1", b, 0]
    parts = [out[i + 1:j] for i, j in zip([-1] + cuts, cuts + [len(out)])]
    return parts[0], parts[1:-1], parts[-1]


class Counts:

    def __init__(self):
        first, self.laps, last = timeline()
        self.first, self.body, self.last = first, self.laps[0], last
        self.n = {}
        count = {}
        marks = [dict(count)]
        for part in [first] + self.laps + [last]:
            for e in part:
                for kind in self.kinds(e):
                    self.n[kind, e] = count.get(kind, 0)
                    count[kind] = count.get(kind, 0) + 1
            marks.append(dict(count))
        self.total = count
        self.per = {k: marks[2].get(k, 0) - marks[1].get(k, 0) for k in count}
        for x, y in zip(self.laps, self.laps[1:]):
            assert [(e[0], e[1] + 1) + e[2:] for e in x] == y

    @staticmethod
    def kinds(e):
        k = [e[0]]
        if e[0] in ACT_JOBS:
            k += ["side", "side_act"]
        if e[0] in DVE_JOBS:
            k += ["side", "side_dve"]
        if e[0].endswith("_stats"):
            k.append("ln")
        if e[0] == "unit" and UNITS[e[3]][1] >= 4 * UNITS[e[3]][0]:
            k.append("diagonal")
        return k


def layer(nc, x, weights, consts, out, q_rows_dram, k_parts_dram):
    plan = Counts()
    LAPS = len(plan.laps)
    ctx = ExitStack()
    with ctx:
        def sb(name, shape, dt=F32):
            return ctx.enter_context(nc.sbuf_tensor(name, shape, dt))

        def pb(name, shape, dt=F32):
            return ctx.enter_context(nc.psum_tensor(name, shape, dt))

        def sem(name):
            return ctx.enter_context(nc.semaphore(name))

        w = sb("w", [P, W_COLS])
        c = sb("c", [P, C_COLS])
        ident = c[:, C_ID:C_ID + P]
        ident_bf = sb("ident_bf", [P, P], BF16)
        minus_half = sb("minus_half", [P, NT])
        one_minus_mu = sb("one_minus_mu", [P, 2])
        xin = sb("xin", [P, NT, D])
        xn = sb("xn", [P, NT, D])
        xnT = sb("xnT", [P, S])
        rot_a = sb("rot_a", [P, 2, HALF])
        rot_b = sb("rot_b", [P, 2, HALF])
        rot = sb("rot", [P, 2, HALF])
        rot_rest = sb("rot_rest", [P, 2, HALF])
        q_parts = sb("q_parts", [P, 3, S], BF16)
        krot_a = sb("krot_a", [64, HALF])
        krot_b = sb("krot_b", [64, HALF])
        krot = sb("krot", [64, HALF])
        krot_rest = sb("krot_rest", [64, HALF])
        k_parts = sb("k_parts", [64, 3, HALF], BF16)
        qs = sb("qs", [P, G, 2, S], BF16)
        k_max_A = sb("k_max_A", [P, 2, S], BF16)
        k_max_B = sb("k_max_B", [P, 2, S], BF16)
        k_main_A = sb("k_main_A", [P, 2, S], BF16)
        k_main_B = sb("k_main_B", [P, 2, S], BF16)
        vA = sb("vA", [P, NT, VW])
        vB = sb("vB", [P, NT, VW])
        tile_max = sb("tile_max", [P, 2, 2, 32])
        row_max = sb("row_max", [P, 2, 32])
        neg_max = sb("neg_max", [P, 2, 32])
        neg_rest = sb("neg_rest", [P, 2, 32])
        m_parts = sb("m_parts", [P, 2, 96], BF16)
        m_rows = sb("m_rows", [96, 2, P], BF16)
        probs = sb("probs", [P, P_RING, 2, HALF])
        o_out = sb("o_out", [P, 2, HALF])
        att = sb("att", [P, 2, 2, HALF])
        recip = sb("recip", [P, 2, HALF])
        attn = sb("attn", [P, 2, HALF])
        xres = sb("xres", [P, NT, D])
        y = sb("y", [P, 2, HALF])
        z = y
        x1 = sb("x1", [P, 2, HALF])
        xn2 = sb("xn2", [P, 2, HALF])
        xn2T = sb("xn2T", [P, S + 1])
        shift = sb("shift", [P, 2, HALF])
        xr = sb("xr", [P, 2, HALF])
        xk = sb("xk", [P, 2, HALF])
        gate = e_neg = sb("e_neg", [P, 2, HALF])
        k_act = k_relu = sb("k_relu", [P, 2, HALF])
        zf = ff = sb("ff", [P, 2, HALF])
        fin = sb("fin", [P, 2, HALF])
        stats = sb("stats", [P, NT, 6])
        mv = sb("mv", [P, NT, 2])
        var_eps = sb("var_eps", [P, NT])
        rstd = sb("rstd", [P, NT])

        score_ps = pb("score_ps", [P, 2, 2, HALF])
        side_ps = pb("side_ps", [P, 2, HALF])
        out_ps = pb("out_ps", [P, 2, HALF])

        w_loaded, c_loaded = sem("w_loaded"), sem("c_loaded")
        x_loaded, xres_loaded = sem("x_loaded"), sem("xres_loaded")
        q_stored, k_stored = sem("q_stored"), sem("k_stored")
        q_loaded = [sem(f"q_loaded{g}") for g in range(G)]
        k_max_A_loaded, k_main_A_loaded = sem("k_max_A_loaded"), sem("k_main_A_loaded")
        kB_loaded = sem("kB_loaded")
        m_loaded = [sem(f"m_loaded{i}") for i in range(2)]
        o_moved = [sem(f"o_moved{i}") for i in range(2)]
        out_stored = [sem(f"out_stored{i}") for i in range(2)]
        k_zero = sem("k_zero")
        q_cleared, k_cleared = sem("q_cleared"), sem("k_cleared")
        consts_set, mu_set = sem("consts_set"), sem("mu_set")
        ln_stats, ln_aggr, ln_eps, ln_rstd = sem("ln_stats"), sem("ln_aggr"), sem("ln_eps"), sem("ln_rstd")
        xn_ready = sem("xn_ready")
        side_ready, side_dve, side_act = sem("side_ready"), sem("side_dve"), sem("side_act")
        q_split_steps, k_split_steps = sem("q_split_steps"), sem("k_split_steps")
        vB_set = sem("vB_set")
        row_max_ready, m_split_steps = sem("row_max_ready"), sem("m_split_steps")
        scores_ready, exp_done, masked = sem("scores_ready"), sem("exp_done"), sem("masked")
        pv_done, o_copied = sem("pv_done"), sem("o_copied")
        ln_sums_ready = sem("ln_sums_ready")
        recip_done, attn_ready = sem("recip_done"), sem("attn_ready")
        z_ready, x1_ready, xn2_ready = sem("z_ready"), sem("x1_ready"), sem("xn2_ready")
        shift_ready, mix_ready = sem("shift_ready"), sem("mix_ready")
        gate_den, gate_ready, k_act_ready = sem("gate_den"), sem("gate_ready"), sem("k_act_ready")
        zf_ready, fin_ready = sem("zf_ready"), sem("fin_ready")

        def upto(kind, e, it, each=1, back=0):
            return each * (plan.n[kind, e] + 1 - back) + each * plan.per[kind] * it

        def in_batch(e, it, per, n):
            return per * e[1] + n + per * it

        def walk(eng, do):
            for e in plan.first:
                do(e, 0)
            for part in plan.laps:
                for e in part:
                    do(e, 0)
            for e in plan.last:
                do(e, 0)

        def batch(e, it):
            return e[1] if isinstance(it, int) and it == 0 else it + e[1]

        def prev(e):
            return (e[0], e[1] - 1) + e[2:]

        def half_cols(h):
            return slice(h * HALF, (h + 1) * HALF)

        def tiles(ap):
            return ap.rearrange("p (t d) -> p t d", d=D)

        block = ctx.enter_context(nc.Block())

        @block.sync
        def _(sp):
            sp.dma_start(xin[:, :, :], x[0].rearrange("(t p) d -> p t d", p=P)).then_inc(x_loaded, 16)
            sp.dma_start(w[:, :], weights[:, :]).then_inc(w_loaded, 16)
            sp.dma_start(c[:, :], consts[:, :]).then_inc(c_loaded, 16)

            def do(e, it):
                kind = e[0]
                if kind == "x_load" and not (e[1] == 0):
                    sp.wait_ge(xn_ready, upto("x_norm", prev(("x_norm", e[1])), it))
                    sp.dma_start(xin[:, :, :], x[batch(e, it)].rearrange("(t p) d -> p t d", p=P))\
                      .then_inc(x_loaded, 16)
                elif kind == "xres_load":
                    if e[1] > 0:
                        sp.wait_ge(x1_ready, upto("x1", ("x1", e[1] - 1, 1), it))
                    sp.dma_start(xres[:, :, :], x[batch(e, it)].rearrange("(t p) d -> p t d", p=P))\
                      .then_inc(xres_loaded, 16)
                elif kind == "k_store":
                    sp.wait_ge(k_split_steps, upto("k_split", ("k_split", e[1], 4), it))
                    if e[1] > 0:
                        sp.wait_ge(k_max_A_loaded, in_batch(e, it, 96, 0))
                    for h in range(2):
                        sp.dma_start(k_parts_dram[:, :, half_cols(h)].rearrange("c d s -> d c s"),
                                     k_parts[32 * h:32 * h + HD, :, :]).then_inc(k_stored, 16)
                elif kind == "kA_load":
                    b = e[1]
                    sp.wait_ge(k_stored, upto("k_store", ("k_store", b), it, each=32))
                    if b == 0:
                        sp.wait_ge(k_cleared, 1)
                    else:
                        sp.wait_ge(side_ready, upto("side", ("max", b - 1, 2, len(MAX_JOBS) - 1), it))
                        sp.wait_ge(scores_ready, upto("unit", ("unit", b - 1, 1, len(UNITS) - 1), it))
                        sp.wait_ge(kB_loaded, in_batch(e, it, 48, 0))
                    for a in range(2):
                        for row, n in ((0, 3), (3, 2), (5, 1)):
                            sp.dma_start(k_max_A[64 * a + HD * row:64 * a + HD * (row + n), a, :],
                                         k_parts_dram[0:n].rearrange("c d s -> (c d) s"))\
                              .then_inc(k_max_A_loaded, 16)
                    sp.wait_ge(k_max_A_loaded, in_batch(e, it, 96, 96))
                    for a in range(2):
                        rows = slice(64 * a, 64 * a + KROWS)
                        sp.dma_start(k_main_A[rows, a, :], k_max_A[rows, a, :]).then_inc(k_main_A_loaded, 16)
                elif kind == "kB_load":
                    b = e[1]
                    if b > 0:
                        sp.wait_ge(side_ready, upto("side", ("max", b - 1, 3, len(MAX_JOBS) - 1), it))
                        sp.wait_ge(scores_ready, upto("unit", ("unit", b - 1, 3, len(UNITS) - 1), it))
                    sp.wait_ge(k_max_A_loaded, in_batch(e, it, 96, 96))
                    sp.dma_start(k_max_B[:, :, :], k_max_A[:, :, :]).then_inc(kB_loaded, 16)
                    for a in range(2):
                        rows = slice(64 * a, 64 * a + KROWS)
                        sp.dma_start(k_main_B[rows, a, :], k_max_A[rows, a, :]).then_inc(kB_loaded, 16)
                elif kind == "q_store":
                    b = e[1]
                    sp.wait_ge(q_split_steps, upto("q_split", ("q_split", b, 1, 4), it))
                    if b > 0:
                        for g in range(G):
                            sp.wait_ge(q_loaded[g], in_batch(e, it, 32, 0))
                    for row, part in enumerate(Q_PART):
                        sp.dma_start(q_rows_dram[:, row], q_parts[:, part, :]).then_inc(q_stored, 16)
                elif kind == "q_load":
                    _, b, g = e
                    sp.wait_ge(q_stored, upto("q_store", ("q_store", b), it, each=16 * len(Q_PART)))
                    if b == 0:
                        sp.wait_ge(q_cleared, 1)
                    else:
                        sp.wait_ge(scores_ready, upto("unit", ("unit", b - 1, g, len(UNITS) - 1), it))
                    for a in range(2):
                        sp.dma_start(qs[64 * a:64 * a + KROWS, g, :, :],
                                     q_rows_dram[G * a + g].rearrange("c (d r) s -> (c d) r s", r=2))\
                          .then_inc(q_loaded[g], 16)
                elif kind == "m_load":
                    _, b, g = e
                    sp.wait_ge(side_act, upto("side_act", ("mT", b, g), it))
                    for a in range(2):
                        sp.dma_start(qs[64 * a + KROWS:64 * a + ROWS, g, :, :],
                                     m_rows[48 * a:48 * a + 48, g % 2, :]).then_inc(m_loaded[g % 2], 16)
                elif kind == "o_copy":
                    _, b, g, qh = e
                    sp.wait_ge(o_copied, upto("o_copy", e, it))
                    if b > 0:
                        sp.wait_ge(attn_ready, upto("o_norm", ("o_norm", b - 1, qh), it))
                    for j in range(4):
                        sp.dma_start(att[32 * g + HD * j:32 * g + HD * (j + 1), qh, :, :],
                                     o_out[32 * j:32 * j + 2 * HD, qh, :]).then_inc(o_moved[qh], 16)
                elif kind == "out":
                    _, b, h = e
                    sp.wait_ge(fin_ready, upto("out", e, it))
                    sp.dma_start(out[batch(e, it)].rearrange("(h t p) d -> h p t d", h=2, p=P)[h],
                                 tiles(fin[:, h, :])).then_inc(out_stored[h], 16)

            walk(sp, do)
            for h in range(2):
                sp.wait_ge(out_stored[h], 16 * B)
            sp.wait_ge(q_stored, 16 * len(Q_PART) * B)
            sp.wait_ge(k_stored, 32 * B)

        @block.tensor
        def _(pe):
            pe.wait_ge(w_loaded, 16)
            pe.wait_ge(c_loaded, 16)
            pe.wait_ge(consts_set, 1)

            def take_side(e, it):
                s = plan.n["side", e]
                users = [u for u in plan_side if plan.n["side", u] == s - 2]
                if users:
                    u = users[0]
                    name = "side_act" if u[0] in ACT_JOBS else "side_dve"
                    pe.wait_ge(side_act if name == "side_act" else side_dve, upto(name, u, it))
                return side_ps[:, s % 2, :]

            plan_side = [e for part in [plan.first] + plan.laps + [plan.last] for e in part
                         if e[0] in ACT_JOBS + DVE_JOBS]

            def do(e, it):
                kind = e[0]
                if kind == "unit":
                    _, b, g, i = e
                    qh, kt, pairs, width = UNITS[i]
                    u = plan.n["unit", e]
                    if i == 0:
                        pe.wait_ge(m_loaded[g % 2], in_batch(e, it, 64, 32 * (g // 2 + 1)))
                        if g == 0:
                            pe.wait_ge(k_main_A_loaded, in_batch(e, it, 32, 32))
                        if g == 2:
                            pe.wait_ge(kB_loaded, in_batch(e, it, 48, 48))
                    if u >= 2:
                        pe.wait_ge(exp_done, upto("unit", e, it, back=2))
                    q0 = (qh + 1) * HALF - width
                    k_main = k_main_A if g < 2 else k_main_B
                    for n, r in enumerate(pairs):
                        for a in range(2):
                            last = nc.tensor.matmul(
                                score_ps[:, u % 2, a, n * width:(n + 1) * width],
                                k_main[:, a, kt * P:(kt + 1) * P],
                                qs[:, g, r, q0:q0 + width], start=True, stop=True)
                    last.then_inc(scores_ready, 1)
                elif kind == "pv":
                    _, b, g, qh, kt = e
                    mine = [("unit", b, g, i) for i, un in enumerate(UNITS) if un[:2] == (qh, kt)]
                    pe.wait_ge(exp_done, upto("unit", mine[-1], it))
                    if kt >= 4 * qh:
                        pe.wait_ge(masked, upto("diagonal", mine[-1], it))
                    if kt == 0:
                        if plan.n["o_copy", ("o_copy", b, g, qh)] >= 2:
                            pe.wait_ge(o_copied, upto("o_copy", ("o_copy", b, g, qh), it, back=2))
                        if qh == 0 and g == 2:
                            pe.wait_ge(vB_set, upto("vB_copy", ("vB_copy", b), it))
                        if qh == 0 and g == 0:
                            pe.wait_ge(side_dve, upto("side_dve", ("v", b, 1), it))
                    v = vA if g < 2 else vB
                    for un in mine:
                        pairs, width = UNITS[un[3]][2:]
                        slot = plan.n["unit", un] % P_RING
                        for n, r in enumerate(pairs):
                            for a in range(2):
                                j = 2 * r + a
                                last = nc.tensor.matmul(
                                    out_ps[32 * j:32 * j + VW, qh, HALF - width:HALF], v[:, kt, :],
                                    probs[:, slot, a, n * width:(n + 1) * width],
                                    start=kt == 0, stop=kt == 4 * qh + 3)
                    last.then_inc(pv_done, 1)
                elif kind == "max":
                    _, b, g, i = e
                    a, pairs, t, k0, n = MAX_JOBS[i]
                    if i == 0:
                        pe.wait_ge(q_loaded[g], in_batch(e, it, 32, 32))
                        if g == 0:
                            pe.wait_ge(k_max_A_loaded, in_batch(e, it, 96, 96))
                        if g == 3:
                            pe.wait_ge(kB_loaded, in_batch(e, it, 48, 48))
                    k_max = k_max_A if g < 3 else k_max_B
                    ps = take_side(e, it)
                    for m, r in enumerate(pairs):
                        last = nc.tensor.matmul(
                            ps[:, m * n:(m + 1) * n], qs[:, g, r, t * P:(t + 1) * P],
                            k_max[:, a, k0:k0 + n], start=True, stop=True)
                    last.then_inc(side_ready, 1)
                elif kind == "mT":
                    _, b, g = e
                    ps = take_side(e, it)
                    pe.wait_ge(m_split_steps, upto("m_split", ("m_split", b, g, 4), it))
                    nc.tensor.transpose(ps.bitcast(BF16)[0:96, 0:P], m_parts[:, g % 2, :], ident_bf[:, :])\
                      .then_inc(side_ready, 1)
                elif kind == "xT":
                    _, b, h = e
                    ps = take_side(e, it)
                    if h == 0:
                        pe.wait_ge(xn_ready, upto("x_norm", ("x_norm", b), it))
                    for t in range(4):
                        last = nc.tensor.transpose(ps[:, t * P:(t + 1) * P], xn[:, 4 * h + t, :], ident)
                    last.then_inc(side_ready, 1)
                elif kind in ("ka", "kb"):
                    b = e[1]
                    ps = take_side(e, it)
                    pe.wait_ge(side_act, upto("side_act", ("xT", b, 1), it))
                    col = W_KA if kind == "ka" else W_KB
                    for h in range(2):
                        last = nc.tensor.matmul(ps[32 * h:32 * h + 32, :], w[:, col:col + 32],
                                                xnT[:, half_cols(h)], start=True, stop=True)
                    last.then_inc(side_ready, 1)
                elif kind in ("qa", "qb"):
                    _, b, h = e
                    ps = take_side(e, it)
                    col = W_QA if kind == "qa" else W_QB
                    nc.tensor.matmul(ps, w[:, col:col + P], xnT[:, half_cols(h)], start=True, stop=True)\
                      .then_inc(side_ready, 1)
                elif kind == "v":
                    _, b, h = e
                    ps = take_side(e, it)
                    for t in range(4):
                        last = nc.tensor.matmul(ps[:, t * HD:(t + 1) * HD], xnT[:, (4 * h + t) * P:(4 * h + t + 1) * P],
                                                w[:, W_V:W_V + HD], start=True, stop=True)
                    last.then_inc(side_ready, 1)
                elif kind in ("y", "r", "f"):
                    _, b, h = e
                    ps = take_side(e, it)
                    src, col = {"y": (attn, W_O), "r": (xr, W_R), "f": (k_act, W_VF)}[kind]
                    if kind == "y":
                        pe.wait_ge(attn_ready, upto("o_norm", ("o_norm", b, h), it))
                    elif kind == "r":
                        pe.wait_ge(mix_ready, upto("mix", ("mix", b, h), it))
                    else:
                        pe.wait_ge(k_act_ready, upto("sq", ("sq", b, h), it))
                    for t in range(4):
                        last = nc.tensor.matmul(ps[:, t * P:(t + 1) * P], src[:, h, t * P:(t + 1) * P],
                                                w[:, col:col + D], start=True, stop=True)
                    last.then_inc(side_ready, 1)
                elif kind == "nT":
                    _, b, h = e
                    ps = take_side(e, it)
                    pe.wait_ge(xn2_ready, upto("x1_norm", ("x1_norm", b, h), it))
                    for t in range(4):
                        last = nc.tensor.transpose(ps[:, t * P:(t + 1) * P], xn2[:, h, t * P:(t + 1) * P], ident)
                    last.then_inc(side_ready, 1)
                elif kind == "k":
                    _, b, h = e
                    ps = take_side(e, it)
                    nc.tensor.matmul(ps, w[:, W_K:W_K + D], xk[:, h, :], start=True, stop=True)\
                      .then_inc(side_ready, 1)

            walk(pe, do)

        @block.scalar
        def _(act):
            nc.scalar.preload_act_table_set("natural_log_exp_and_others")

            def do(e, it):
                kind = e[0]
                if kind == "unit":
                    _, b, g, i = e
                    qh, kt, pairs, width = UNITS[i]
                    u = plan.n["unit", e]
                    n = len(pairs) * width
                    old = [x for x in all_units if plan.n["unit", x] == u - P_RING]
                    if old:
                        o = old[0]
                        act.wait_ge(pv_done, upto("pv", ("pv", o[1], o[2]) + UNITS[o[3]][:2], it))
                    act.wait_ge(scores_ready, upto("unit", e, it))
                    nc.scalar.activation(probs[:, u % P_RING, :, 0:n], score_ps[:, u % 2, :, 0:n],
                                         ACT.Exp, scale=SCALE).then_inc(exp_done, 1)
                elif kind == "o_copy":
                    _, b, g, qh = e
                    act.wait_ge(pv_done, upto("pv", ("pv", b, g, qh, 4 * qh + 3), it))
                    if plan.n["o_copy", e] >= 2:
                        act.wait_ge(o_moved[qh], in_batch(e, it, 256, 64 * g))
                    nc.scalar.activation(o_out[:, qh, :], out_ps[:, qh, :], ACT.Copy).then_inc(o_copied, 1)
                elif kind == "o_norm":
                    _, b, h = e
                    act.wait_ge(o_moved[h], in_batch(e, it, 256, 256))
                    nc.scalar.activation(recip[:, h, :], att[:, h, 1, :], ACT.Ln).then_inc(ln_sums_ready, 1)
                    act.wait_ge(ln_sums_ready, upto("o_norm", e, it))
                    nc.scalar.activation(recip[:, h, :], recip[:, h, :], ACT.Exp, scale=-1.0)\
                      .then_inc(recip_done, 1)
                elif kind in ACT_JOBS:
                    ps = side_ps[:, plan.n["side", e] % 2, :]
                    act.wait_ge(side_ready, upto("side", e, it))
                    if kind == "mT":
                        if plan.n["mT", e] >= 2:
                            act.wait_ge(m_loaded[e[2] % 2], in_batch(e, it, 64, 32 * (e[2] // 2)))
                        nc.scalar.activation(m_rows[:, e[2] % 2, :], ps.bitcast(BF16)[0:96, 0:P], ACT.Copy)\
                          .then_inc(side_act, 1)
                        return
                    h = e[2]
                    if kind == "xT":
                        dst, func, scale = xnT[:, half_cols(h)], ACT.Copy, 1.0
                    elif kind == "y":
                        dst, func, scale = y[:, h, :], ACT.Copy, 1.0
                    elif kind == "nT":
                        dst, func, scale = xn2T[:, 1 + h * HALF:1 + (h + 1) * HALF], ACT.Copy, 1.0
                    elif kind == "r":
                        dst, func, scale = e_neg[:, h, :], ACT.Exp, -1.0
                    else:
                        dst, func, scale = k_relu[:, h, :], ACT.Relu, 1.0
                    nc.scalar.activation(dst, ps, func, scale=scale).then_inc(side_act, 1)

            all_units = [e for part in [plan.first] + plan.laps + [plan.last] for e in part if e[0] == "unit"]
            walk(act, do)

        @block.vector
        def _(dve):
            for k in (k_max_A, k_main_A, k_main_B):
                nc.vector.memset(k[:, :, :].bitcast(F32), 0.0).then_inc(k_zero, 1)
            dve.wait_ge(k_zero, 3)
            for k in (k_main_A, k_main_B):
                nc.vector.memset(k[32:64, 0, :], 1.0)
                last = nc.vector.memset(k[96:128, 1, :], 1.0)
            last.then_inc(k_cleared, 1)
            for v in (vA, vB):
                nc.vector.memset(v[:, :, 0:2 * HD].rearrange("p t (d w) -> p t d w", w=2)[:, :, :, 1], 1.0)
                nc.vector.memset(v[:, :, 2 * HD:VW], 0.0)
            nc.vector.memset(tile_max[:, :, 0, :], LOWEST)
            nc.vector.memset(xn2T[:, 0:1], 0.0)
            dve.wait_ge(c_loaded, 16)
            nc.vector.tensor_copy(ident_bf[:, :], ident).then_inc(consts_set, 1)
            dve.wait_ge(w_loaded, 16)
            nc.vector.tensor_scalar(one_minus_mu[:, :], w[:, W_MU:W_MU + 2], -1.0, 1.0, ALU.mult, ALU.add)\
              .then_inc(mu_set, 1)
            dve.wait_ge(mu_set, 1)

            def norm_stats(src, n, e, it):
                for t in range(n):
                    last = nc.vector.bn_stats(stats[:, t, :], src[:, t, :])
                last.then_inc(ln_stats, 1)
                dve.wait_ge(ln_stats, upto("ln", e, it))
                for t in range(n):
                    last = nc.vector.bn_aggr(mv[:, t, :], stats[:, t, :])
                last.then_inc(ln_aggr, 1)

            def norm_apply(dst, src, n, e, it, done):
                dve.wait_ge(ln_rstd, upto("ln", e, it))
                for t in range(n):
                    last = nc.vector.tensor_scalar(dst[:, t, :], src[:, t, :], mv[:, t, 0:1], rstd[:, t:t + 1],
                                                   ALU.subtract, ALU.mult)
                last.then_inc(done, 1)

            def do(e, it):
                kind = e[0]
                if kind == "max":
                    _, b, g, i = e
                    a, pairs, t, k0, n = MAX_JOBS[i]
                    ps = side_ps[:, plan.n["side", e] % 2, :]
                    if i == 0 and plan.n["m_max", ("m_max", b, g)] >= 2:
                        dve.wait_ge(row_max_ready, upto("m_max", ("m_max", b, g), it, back=2))
                    dve.wait_ge(side_ready, upto("side", e, it))
                    for m, r in enumerate(pairs):
                        col = 16 * a + 8 * r + t
                        seg = ps[:, m * n:(m + 1) * n]
                        if k0 + n <= t * P:
                            last = nc.vector.tensor_reduce(out=tile_max[:, g % 2, 0, col:col + 1], in_=seg,
                                                           axis=AX_X, op=ALU.max)
                        else:
                            last = nc.vector.tensor_tensor_reduce(
                                out=seg, in0=seg, in1=c[:, C_MASK + HALF - n:C_MASK + HALF], scale=1.0,
                                scalar=LOWEST, op0=ALU.add, op1=ALU.max,
                                accum_out=tile_max[:, g % 2, 1, col:col + 1])
                    last.then_inc(side_dve, 1)
                elif kind == "m_max":
                    _, b, g = e
                    dve.wait_ge(side_dve, upto("side_dve", ("max", b, g, len(MAX_JOBS) - 1), it))
                    if plan.n["m_max", e] >= 2:
                        dve.wait_ge(m_split_steps, upto("m_split", ("m_split", b, g, 4), it, back=10))
                    nc.vector.tensor_tensor(row_max[:, g % 2, :], tile_max[:, g % 2, 0, :],
                                            tile_max[:, g % 2, 1, :], ALU.max).then_inc(row_max_ready, 1)
                elif kind == "x_stats":
                    dve.wait_ge(x_loaded, upto("x_load", ("x_load", e[1]), it, each=16))
                    norm_stats(xin, NT, e, it)
                elif kind == "x_norm":
                    norm_apply(xn, xin, NT, ("x_stats", e[1]), it, xn_ready)
                elif kind in ("qa", "qb"):
                    _, b, h = e
                    dve.wait_ge(side_ready, upto("side", e, it))
                    dst, col = (rot_a, C_COS) if kind == "qa" else (rot_b, C_SIN)
                    nc.vector.tensor_tensor(dst[:, h, :], side_ps[:, plan.n["side", e] % 2, :],
                                            c[:, col + h * HALF:col + (h + 1) * HALF], ALU.mult)\
                      .then_inc(side_dve, 1)
                elif kind in ("ka", "kb"):
                    dve.wait_ge(side_ready, upto("side", e, it))
                    dst, col = (krot_a, C_KCOS) if kind == "ka" else (krot_b, C_KSIN)
                    nc.vector.tensor_tensor(dst[:, :], side_ps[0:64, plan.n["side", e] % 2, :],
                                            c[0:64, col:col + HALF], ALU.mult).then_inc(side_dve, 1)
                elif kind == "v":
                    _, b, h = e
                    if h == 0 and b > 0:
                        dve.wait_ge(vB_set, upto("vB_copy", ("vB_copy", b - 1), it))
                        dve.wait_ge(pv_done, upto("pv", ("pv", b - 1, 1, 1, 7), it))
                    dve.wait_ge(side_ready, upto("side", e, it))
                    nc.vector.tensor_copy(vA[:, 4 * h:4 * h + 4, 0:2 * HD:2],
                                          side_ps[:, plan.n["side", e] % 2, 0:4 * HD]
                                          .rearrange("p (t d) -> p t d", d=HD)).then_inc(side_dve, 1)
                elif kind == "o_norm":
                    _, b, h = e
                    dve.wait_ge(recip_done, upto("o_norm", e, it))
                    nc.vector.tensor_tensor(attn[:, h, :], att[:, h, 0, :], recip[:, h, :], ALU.mult)\
                      .then_inc(attn_ready, 1)
                elif kind == "y_stats":
                    dve.wait_ge(side_act, upto("side_act", ("y", e[1], e[2]), it))
                    norm_stats(tiles(y[:, e[2], :]), 4, e, it)
                elif kind == "y_norm":
                    norm_apply(tiles(z[:, e[2], :]), tiles(y[:, e[2], :]), 4, ("y_stats",) + e[1:], it, z_ready)
                elif kind == "x1_stats":
                    dve.wait_ge(x1_ready, upto("x1", ("x1", e[1], e[2]), it))
                    norm_stats(tiles(x1[:, e[2], :]), 4, e, it)
                elif kind == "x1_norm":
                    norm_apply(tiles(xn2[:, e[2], :]), tiles(x1[:, e[2], :]), 4, ("x1_stats",) + e[1:], it,
                               xn2_ready)
                elif kind == "mix":
                    _, b, h = e
                    dve.wait_ge(shift_ready, upto("diff", ("diff", b, h), it))
                    for n, dst in enumerate((xr, xk)):
                        last = nc.vector.scalar_tensor_tensor(
                            out=dst[:, h, :], in0=shift[:, h, :], scalar=one_minus_mu[:, n:n + 1],
                            in1=xn2T[:, 1 + h * HALF:1 + (h + 1) * HALF], op0=ALU.mult, op1=ALU.add)
                    last.then_inc(mix_ready, 1)
                elif kind == "sig":
                    _, b, h = e
                    dve.wait_ge(side_act, upto("side_act", ("r", b, h), it))
                    nc.vector.tensor_scalar_add(e_neg[:, h, :], e_neg[:, h, :], 1.0).then_inc(gate_den, 1)
                    dve.wait_ge(gate_den, upto("sig", e, it))
                    nc.vector.reciprocal(gate[:, h, :], e_neg[:, h, :]).then_inc(gate_ready, 1)
                elif kind == "f":
                    _, b, h = e
                    dve.wait_ge(gate_ready, upto("sig", ("sig", b, h), it))
                    dve.wait_ge(side_ready, upto("side", e, it))
                    nc.vector.tensor_tensor(ff[:, h, :], side_ps[:, plan.n["side", e] % 2, :], gate[:, h, :],
                                            ALU.mult).then_inc(side_dve, 1)
                elif kind == "f_stats":
                    dve.wait_ge(side_dve, upto("side_dve", ("f", e[1], e[2]), it))
                    norm_stats(tiles(ff[:, e[2], :]), 4, e, it)
                elif kind == "f_norm":
                    norm_apply(tiles(zf[:, e[2], :]), tiles(ff[:, e[2], :]), 4, ("f_stats",) + e[1:], it, zf_ready)

            walk(dve, do)

        @block.gpsimd
        def _(pool):
            nc.gpsimd.memset(minus_half[:, :], -0.5)
            nc.gpsimd.memset(qs[:, :, :, :].bitcast(F32), 0.0).then_inc(q_cleared, 1)

            def split_step(i, src_a, src_b, whole, rest, parts, s, kind, e, it):
                if i > 0:
                    pool.wait_ge(s, upto(kind, e, it, back=1))
                if i == 0:
                    op = nc.gpsimd.tensor_tensor(out=whole, in0=src_a, in1=src_b, op=ALU.add)
                elif i == 1:
                    op = nc.gpsimd.tensor_copy(parts[0], whole)
                elif i == 2:
                    op = nc.gpsimd.tensor_tensor(out=rest, in0=whole, in1=parts[0], op=ALU.subtract)
                elif i == 3:
                    op = nc.gpsimd.tensor_copy(parts[1], rest)
                else:
                    op = nc.gpsimd.tensor_tensor(out=parts[2], in0=rest, in1=parts[1], op=ALU.subtract)
                op.then_inc(s, 1)

            def rstd_of(n, e, it):
                pool.wait_ge(ln_aggr, upto("ln", e, it))
                nc.gpsimd.tensor_scalar(out=var_eps[:, 0:n], in0=mv[:, 0:n, 1], scalar1=EPS, scalar2=None,
                                        op0=ALU.add).then_inc(ln_eps, 1)
                pool.wait_ge(ln_eps, upto("ln", e, it))
                nc.gpsimd.tensor_tensor(out=rstd[:, 0:n], in0=var_eps[:, 0:n], in1=minus_half[:, 0:n],
                                        op=ALU.pow).then_inc(ln_rstd, 1)

            def do(e, it):
                kind = e[0]
                if kind == "unit":
                    _, b, g, i = e
                    qh, kt, pairs, width = UNITS[i]
                    if kt < 4 * qh:
                        return
                    u = plan.n["unit", e]
                    pool.wait_ge(exp_done, upto("unit", e, it))
                    if len(pairs) == 1:
                        d = probs[:, u % P_RING, :, 0:P]
                        pattern = [[0, 2], [1, P]]
                    else:
                        d = probs[:, u % P_RING, :, 0:2 * width].rearrange("p a (r q) -> p a r q", r=2)[:, :, :, 0:P]
                        pattern = [[0, 2], [0, 2], [1, P]]
                    nc.gpsimd.affine_select(out=d, in_=d, pattern=pattern, compare_op=ALU.is_ge, fill=0.0,
                                            base=0, channel_multiplier=-1).then_inc(masked, 1)
                elif kind == "q_split":
                    _, b, h, i = e
                    if i == 0:
                        pool.wait_ge(side_dve, upto("side_dve", ("qb", b, h), it))
                        if b > 0:
                            pool.wait_ge(q_stored, upto("q_store", ("q_store", b - 1), it, each=96))
                    split_step(i, rot_a[:, h, :], rot_b[:, h, :], rot[:, h, :], rot_rest[:, h, :],
                               [q_parts[:, n, half_cols(h)] for n in range(3)], q_split_steps, kind, e, it)
                elif kind == "k_split":
                    _, b, i = e
                    if i == 0:
                        pool.wait_ge(side_dve, upto("side_dve", ("kb", b), it))
                        if b > 0:
                            pool.wait_ge(k_stored, upto("k_store", ("k_store", b - 1), it, each=32))
                    split_step(i, krot_a[:, :], krot_b[:, :], krot[:, :], krot_rest[:, :],
                               [k_parts[:, n, :] for n in range(3)], k_split_steps, kind, e, it)
                elif kind == "m_split":
                    _, b, g, i = e
                    par = g % 2
                    parts = [m_parts[:, par, :].rearrange("p (a n x) -> p a n x", a=2, n=3)[:, :, n, :]
                             for n in range(3)]
                    whole, rest = (m[:, par, :].rearrange("p (a x) -> p a x", a=2) for m in (neg_max, neg_rest))
                    if i == 0:
                        pool.wait_ge(row_max_ready, upto("m_max", ("m_max", b, g), it))
                        if plan.n["mT", ("mT", b, g)] >= 2:
                            pool.wait_ge(side_act, upto("side_act", MT[plan.n["mT", ("mT", b, g)] - 2], it))
                        nc.gpsimd.tensor_scalar(out=neg_max[:, par, :], in0=row_max[:, par, :], scalar1=-1.0,
                                                scalar2=None, op0=ALU.mult).then_inc(m_split_steps, 1)
                    else:
                        split_step(i, None, None, whole, rest, parts,
                                   m_split_steps, kind, e, it)
                elif kind == "vB_copy":
                    b = e[1]
                    pool.wait_ge(side_dve, upto("side_dve", ("v", b, 1), it))
                    if b > 0:
                        pool.wait_ge(pv_done, upto("pv", ("pv", b - 1, 3, 1, 7), it))
                    nc.gpsimd.tensor_copy(vB[:, :, 0:2 * HD:2], vA[:, :, 0:2 * HD:2]).then_inc(vB_set, 1)
                elif kind.endswith("_stats"):
                    rstd_of(NT if kind == "x_stats" else 4, e, it)
                elif kind == "x1":
                    _, b, h = e
                    pool.wait_ge(z_ready, upto("y_norm", ("y_norm", b, h), it))
                    pool.wait_ge(xres_loaded, upto("xres_load", ("xres_load", b), it, each=16))
                    nc.gpsimd.tensor_tensor(out=tiles(x1[:, h, :]), in0=tiles(z[:, h, :]),
                                            in1=xres[:, 4 * h:4 * h + 4, :], op=ALU.add).then_inc(x1_ready, 1)
                elif kind == "diff":
                    _, b, h = e
                    pool.wait_ge(side_act, upto("side_act", ("nT", b, h), it))
                    nc.gpsimd.tensor_tensor(out=shift[:, h, :], in0=xn2T[:, h * HALF:(h + 1) * HALF],
                                            in1=xn2T[:, 1 + h * HALF:1 + (h + 1) * HALF], op=ALU.subtract)\
                      .then_inc(shift_ready, 1)
                elif kind == "sq":
                    _, b, h = e
                    pool.wait_ge(side_act, upto("side_act", ("k", b, h), it))
                    nc.gpsimd.tensor_tensor(out=k_act[:, h, :], in0=k_relu[:, h, :], in1=k_relu[:, h, :],
                                            op=ALU.mult).then_inc(k_act_ready, 1)
                elif kind == "out":
                    _, b, h = e
                    pool.wait_ge(zf_ready, upto("f_norm", ("f_norm", b, h), it))
                    if b > 0:
                        pool.wait_ge(out_stored[h], in_batch(e, it, 16, 0))
                    nc.gpsimd.tensor_tensor(out=fin[:, h, :], in0=zf[:, h, :], in1=x1[:, h, :], op=ALU.add)\
                      .then_inc(fin_ready, 1)

            MT = [e for part in [plan.first] + plan.laps + [plan.last] for e in part if e[0] == "mT"]
            walk(pool, do)



def rotary_order():
    half = HD // 2
    near = [2 * i for i in range(half)] + [2 * i + 1 for i in range(half)]
    far = [2 * i + 1 for i in range(half)] + [2 * i for i in range(half)]
    return near, far


def constant_array():
    half = HD // 2
    freqs = (np.float32(1.0) / np.float32(THETA) ** (np.arange(0, HD, 2, dtype=np.float32) / np.float32(HD)))
    ang = np.arange(S, dtype=np.float32)[:, None] * freqs.astype(np.float32)[None, :]
    cos, sin = np.cos(ang).astype(np.float32), np.sin(ang).astype(np.float32)
    cos8 = np.concatenate([cos, cos], axis=1).T
    sin8 = np.concatenate([-sin, sin], axis=1).T
    c = np.zeros((P, C_COLS), np.float32)
    c[:, C_ID:C_ID + P] = np.eye(P, dtype=np.float32)
    c[:, C_MASK + HALF - P:C_MASK + HALF] = np.where(np.arange(P)[None, :] > np.arange(P)[:, None], NEG, 0.0)
    for h in range(2):
        c[32 * h:32 * h + HD, C_KCOS:C_KCOS + HALF] = cos8[:, h * HALF:(h + 1) * HALF]
        c[32 * h:32 * h + HD, C_KSIN:C_KSIN + HALF] = sin8[:, h * HALF:(h + 1) * HALF]
    c[:, C_COS:C_COS + S] = np.tile(np.repeat(cos8, 2, axis=0), (P // (2 * HD), 1))
    c[:, C_SIN:C_SIN + S] = np.tile(np.repeat(sin8, 2, axis=0), (P // (2 * HD), 1))
    return c


def weight_array(wq, wk, wv, wo, w_r, w_k, w_v, mu_r, mu_k):
    near, far = rotary_order()
    w = np.zeros((P, W_COLS), np.float32)
    for col, order in ((W_QA, near), (W_QB, far)):
        rows = [HD * (4 * g + 2 * r + a) + d for a in range(2) for g in range(G) for d in order for r in range(2)]
        w[:, col:col + P] = wq[rows, :].T
    w[:, W_KA:W_KA + HD] = wk[:, near]
    w[:, W_KB:W_KB + HD] = wk[:, far]
    w[:, W_V:W_V + HD] = wv
    w[:, W_O:W_O + D] = wo.T
    w[:, W_R:W_R + D] = w_r.T
    w[:, W_K:W_K + D] = w_k.T
    w[:, W_VF:W_VF + D] = w_v.T
    w[:, W_MU] = mu_r
    w[:, W_MU + 1] = mu_k
    return w


def kernel(L0_attn_x, L0_attn_wq, L0_attn_wk, L0_attn_wv, L0_attn_wo, L0_ffn_W_r, L0_ffn_W_k,
           L0_ffn_W_v, L0_ffn_mu_r, L0_ffn_mu_k):
    import concourse.bacc as bacc
    from concourse.bass_utils import run_bass_kernel_spmd

    a = np.asarray
    arrays = {
        "x": np.ascontiguousarray(a(L0_attn_x)),
        "weights": weight_array(a(L0_attn_wq), a(L0_attn_wk), a(L0_attn_wv), a(L0_attn_wo), a(L0_ffn_W_r),
                                a(L0_ffn_W_k), a(L0_ffn_W_v), a(L0_ffn_mu_r), a(L0_ffn_mu_k)),
        "consts": constant_array(),
    }
    nc = bacc.Bacc("TRN2", target_bir_lowering=False, num_devices=1)
    ins = {n: nc.dram_tensor(n, v.shape, F32, kind="ExternalInput").ap() for n, v in arrays.items()}
    out = nc.dram_tensor("out", (B, S, D), F32, kind="ExternalOutput").ap()
    q_dram = nc.dram_tensor("q_rows_dram", (2 * G, len(Q_PART), 2 * HD, S), BF16, kind="Internal").ap()
    k_dram = nc.dram_tensor("k_parts_dram", (3, HD, S), BF16, kind="Internal").ap()
    layer(nc, ins["x"], ins["weights"], ins["consts"], out, q_dram, k_dram)
    result = run_bass_kernel_spmd(nc, [arrays], core_ids=[0])
    return result.results[0]["out"]
```

```python
from contextlib import ExitStack

import numpy as np

import concourse.bass as bass
from concourse import mybir

F32 = mybir.dt.float32
BF16 = mybir.dt.bfloat16
ALU = mybir.AluOpType
ACT = mybir.ActivationFunctionType
AX_X = mybir.AxisListType.X

P = 128
B, S, D = 4, 1024, 128
H, HD = 16, 8
THETA = 1000.0
EPS = 1e-5
NT = S // P
HALF = S // 2
G = 4
SCALE = 1.0 / float(np.sqrt(HD))
NEG = -1e30
LOWEST = -3e38
Q_PART = (0, 0, 0, 1, 1, 2)
K_PART = (0, 1, 2, 0, 1, 0)
KROWS = 8 * len(Q_PART)
ROWS = KROWS + 3
VW = 32
P_RING = 4
S_RING = 3
SIDE_BANKS = 4
LAG = 5
EVAC_LAG = 1

W_QA, W_QB, W_KA, W_KB, W_V = 0, 128, 256, 288, 320
W_O, W_R, W_K, W_VF, W_MU = 328, 456, 584, 712, 840
W_COLS = 842
C_ID, C_MASK, C_KCOS, C_KSIN, C_COS, C_SIN = 0, 128, 1152, 1664, 2176, 3200
C_COLS = 4224



def main_units():
    out = []
    for qh in range(2):
        for kt in range(4 * (qh + 1)):
            width = HALF - P * max(0, kt - 4 * qh)
            n = max(1, min(4, HALF // width)) if width != 384 else 1
            out += [(qh, kt, tuple(range(j, j + n)), width) for j in range(0, 4, n)]
    return out


UNITS = main_units()


def max_jobs():
    out = []
    for t in range(NT):
        n = (4, 2, 1, 1)[t] if t < 4 else 1
        out += [(t, tuple(range(j, j + n))) for j in range(0, 4, n)]
    return out


MAX_JOBS = max_jobs()

ACT_JOBS = ("xT", "mT", "y", "nT", "r", "k")
DVE_JOBS = ("max", "qa", "qb", "ka", "kb", "v", "f")

GROUP = 1000
BATCH = G * GROUP
MAIN_AT = 1400
CLOSE = (10, 250)


def spread(items, start, end):
    return [(start + (end - start) * i // max(1, len(items) - 1), e) for i, e in enumerate(items)]


def pre_items(b):
    z = BATCH * b
    split_k = [("k_split", b, i) for i in range(5)]
    split_q = [[("q_split", b, h, i) for i in range(5)] for h in range(2)]
    out = spread([("x_load", b), ("x_stats", b), ("x_norm", b), ("xT", b, 0), ("xT", b, 1), ("ka", b), ("kb", b),
                  ("qa", b, 0), ("qb", b, 0)]
                 + split_k + [("k_store", b)] + split_q[0] + [("qa", b, 1), ("qb", b, 1)] + split_q[1]
                 + [("q_store", b)], z - 1500, z - 500)
    out += [(z - 500, ("k_max_load", b)), (z - 450, ("q_load", b, 0)), (z - 400, ("k_main_load", b)),
            (z - 300, ("q_load", b, 1)), (z - 300, ("v", b, 0)), (z - 250, ("v", b, 1))]
    return out


def post_items(b, h):
    items = [("y", b, h), ("y_stats", b, h), ("y_norm", b, h), ("x1", b, h),
             ("x1_stats", b, h), ("x1_norm", b, h), ("nT", b, h), ("diff", b, h), ("mix", b, h),
             ("r", b, h), ("k", b, h), ("sq", b, h), ("sig", b, h), ("f", b, h), ("f_stats", b, h),
             ("f_norm", b, h), ("out", b, h)]
    begin = BATCH * b + (4850 if h == 0 else 5650)
    return [(begin, ("o_norm", b, h))] + spread(items, begin + 80, begin + 840)


def timeline():
    keyed = []
    cost = [n * (65 + 1.04 * P * (t + 1)) for t, hs in MAX_JOBS for n in [len(hs)]]
    cols = [len(hs) * width for _, _, hs, width in UNITS]
    for b in range(B):
        keyed += pre_items(b) + post_items(b, 0) + post_items(b, 1)
        for g in range(G):
            z = BATCH * b + GROUP * g
            keyed += [(z + int(GROUP * sum(cost[:i]) / sum(cost)), ("max", b, g, i))
                      for i in range(len(MAX_JOBS))]
            keyed += spread([("m_split", b, g, i) for i in range(5)] + [("mT", b, g), ("m_load", b, g)],
                            z + GROUP + CLOSE[0], z + GROUP + CLOSE[1])
            m = z + MAIN_AT
            keyed += [(m + GROUP * sum(cols[:i]) // sum(cols), ("unit", b, g, i))
                      for i in range(len(UNITS))]
            if g >= 2 and b + 1 < B:
                keyed.append((m + GROUP, ("q_load", b + 1, g)))
            if b == 0 and g >= 2:
                keyed.append((100 * g, ("q_load", 0, g)))
        keyed.append((BATCH * b + 4000, ("xres_load", b)))
        keyed.append((BATCH * b + 1900 if b > 0 else 500, ("vB_copy", b)))
        keyed.append((BATCH * b + MAIN_AT if b > 0 else 600, ("kB_load", b)))
        keyed.append((BATCH * b + 2500, ("loop",)))
    raw = [e for _, e in sorted(keyed, key=lambda x: (x[0], x[1] != ("loop",), x[1]))]
    out, pending, n = [], [], 0
    for e in raw:
        out.append(e)
        if e[0] != "unit":
            continue
        n += 1
        _, b, g, i = e
        qh, kt, _, _ = UNITS[i]
        if i + 1 == len(UNITS) or UNITS[i + 1][:2] != (qh, kt):
            pending.append((n + LAG, ("pv", b, g, qh, kt)))
            if kt == 4 * qh + 3:
                pending.append((n + LAG + EVAC_LAG, ("o_copy", b, g, qh)))
        while pending and min(pending)[0] <= n:
            nxt = min(pending)
            pending.remove(nxt)
            out.append(nxt[1])
    assert not pending or raw[-1][0] != "unit"
    if pending:
        where = max(i for i, e in enumerate(out) if e[0] == "unit") + 1
        out[where:where] = [nxt[1] for nxt in sorted(pending)]
    cuts = [i for i, e in enumerate(out) if e == ("loop",)]
    place = {e: n for n, e in enumerate(out)}
    for b in range(B):
        for g in range(G):
            assert place["m_load", b, g] < place["unit", b, g, 0], (b, g)
        for h in range(2):
            assert place["o_copy", b, 3, h] < place["o_norm", b, h], (b, h)
        assert place["xres_load", b] < place["x1", b, 0]
    parts = [out[i + 1:j] for i, j in zip([-1] + cuts, cuts + [len(out)])]
    return parts[0], parts[1:-1], parts[-1]


def last_of_set(i):
    return i + 1 == len(UNITS) or UNITS[i + 1][:2] != UNITS[i][:2]


def set_end(i):
    while not last_of_set(i):
        i += 1
    return i


class Counts:

    def __init__(self):
        first, self.laps, last = timeline()
        self.first, self.body, self.last = first, self.laps[0], last
        self.n = {}
        count = {}
        marks = [dict(count)]
        for part in [first] + self.laps + [last]:
            for e in part:
                for kind in self.kinds(e):
                    self.n[kind, e] = count.get(kind, 0)
                    count[kind] = count.get(kind, 0) + 1
            marks.append(dict(count))
        self.total = count
        self.place_side_tiles([first] + self.laps + [last])
        self.per = {k: marks[2].get(k, 0) - marks[1].get(k, 0) for k in count}
        for x, y in zip(self.laps, self.laps[1:]):
            assert [(e[0], e[1] + 1) + e[2:] for e in x] == y

    def place_side_tiles(self, parts):
        self.bank, self.before, owner = {}, {}, {}
        for part in parts:
            at_bank = 0
            for e in part:
                if e[0] not in ACT_JOBS + DVE_JOBS:
                    continue
                wide = e[0] == "max" and MAX_JOBS[e[3]][0] >= 4
                if wide:
                    at_bank = (at_bank + 1) // 2 * 2 % SIDE_BANKS
                banks = range(at_bank, at_bank + 1 + wide)
                self.bank[e] = at_bank
                self.before[e] = sorted({owner[k] for k in banks if k in owner}, key=lambda u: self.n["side", u])
                for k in banks:
                    owner[k] = e
                at_bank = (at_bank + 1 + wide) % SIDE_BANKS

    @staticmethod
    def kinds(e):
        k = [e[0]]
        if e[0] in ACT_JOBS:
            k += ["side", "side_act"]
        if e[0] in DVE_JOBS:
            k += ["side", "side_dve"]
        if e[0].endswith("_stats"):
            k.append("ln")
        if e[0] == "unit" and last_of_set(e[3]):
            k.append("set")
            if UNITS[e[3]][1] >= 4 * UNITS[e[3]][0]:
                k.append("diagonal")
        return k


def layer(nc, x, weights, consts, out, q_rows_dram, k_parts_dram):
    plan = Counts()
    LAPS = len(plan.laps)
    ctx = ExitStack()
    with ctx:
        def sb(name, shape, dt=F32):
            return ctx.enter_context(nc.sbuf_tensor(name, shape, dt))

        def pb(name, shape, dt=F32):
            return ctx.enter_context(nc.psum_tensor(name, shape, dt))

        def sem(name):
            return ctx.enter_context(nc.semaphore(name))

        w = sb("w", [P, W_COLS])
        c = sb("c", [P, C_COLS])
        ident = c[:, C_ID:C_ID + P]
        ident_bf = sb("ident_bf", [P, P], BF16)
        minus_half = sb("minus_half", [P, NT])
        one_minus_mu = sb("one_minus_mu", [P, 2])
        xin = sb("xin", [P, NT, D])
        xn = sb("xn", [P, NT, D])
        xnT = sb("xnT", [P, S])
        rot_a = sb("rot_a", [P, 2, HALF])
        rot_b = sb("rot_b", [P, 2, HALF])
        rot = sb("rot", [P, 2, HALF])
        rot_rest = sb("rot_rest", [P, 2, HALF])
        q_parts = sb("q_parts", [P, 3, S], BF16)
        krot_a = sb("krot_a", [64, HALF])
        krot_b = sb("krot_b", [64, HALF])
        krot = sb("krot", [64, HALF])
        krot_rest = sb("krot_rest", [64, HALF])
        k_parts = sb("k_parts", [64, 3, HALF], BF16)
        qs = sb("qs", [P, G, 2, S], BF16)
        k_max_A = sb("k_max_A", [P, 2, S], BF16)
        k_max_B = sb("k_max_B", [P, 2, S], BF16)
        k_main_A = sb("k_main_A", [P, 2, S], BF16)
        k_main_B = sb("k_main_B", [P, 2, S], BF16)
        vA = sb("vA", [P, NT, VW])
        vB = sb("vB", [P, NT, VW])
        row_max = sb("row_max", [P, 2, 32])
        neg_max = sb("neg_max", [P, 2, 32])
        neg_rest = sb("neg_rest", [P, 2, 32])
        m_parts = sb("m_parts", [P, 2, 96], BF16)
        m_rows = sb("m_rows", [96, 2, P], BF16)
        probs = sb("probs", [P, P_RING, 4 * HALF])
        o_out = sb("o_out", [P, 2, HALF])
        att = sb("att", [P, 2, 2, HALF])
        recip = sb("recip", [P, 2, HALF])
        attn = sb("attn", [P, 2, HALF])
        xres = sb("xres", [P, NT, D])
        y = sb("y", [P, 2, HALF])
        z = y
        x1 = sb("x1", [P, 2, HALF])
        xn2 = sb("xn2", [P, 2, HALF])
        xn2T = sb("xn2T", [P, S + 1])
        shift = sb("shift", [P, 2, HALF])
        xr = sb("xr", [P, 2, HALF])
        xk = sb("xk", [P, 2, HALF])
        gate = e_neg = sb("e_neg", [P, 2, HALF])
        k_act = k_relu = sb("k_relu", [P, 2, HALF])
        zf = ff = sb("ff", [P, 2, HALF])
        fin = sb("fin", [P, 2, HALF])
        stats = sb("stats", [P, NT, 6])
        mv = sb("mv", [P, NT, 2])
        var_eps = sb("var_eps", [P, NT])
        rstd = sb("rstd", [P, NT])

        score_ps = pb("score_ps", [P, S_RING, HALF])
        side_ps = pb("side_ps", [P, SIDE_BANKS * HALF])
        out_ps = pb("out_ps", [P, HALF])

        w_loaded, c_loaded = sem("w_loaded"), sem("c_loaded")
        x_loaded, xres_loaded = sem("x_loaded"), sem("xres_loaded")
        q_stored, k_stored = sem("q_stored"), sem("k_stored")
        q_loaded = [sem(f"q_loaded{g}") for g in range(G)]
        k_max_A_loaded, k_main_A_loaded = sem("k_max_A_loaded"), sem("k_main_A_loaded")
        kB_loaded = sem("kB_loaded")
        m_loaded = [sem(f"m_loaded{i}") for i in range(2)]
        o_moved = [sem(f"o_moved{i}") for i in range(2)]
        out_stored = [sem(f"out_stored{i}") for i in range(2)]
        k_zero = sem("k_zero")
        q_cleared, k_cleared = sem("q_cleared"), sem("k_cleared")
        consts_set, mu_set = sem("consts_set"), sem("mu_set")
        ln_stats, ln_aggr, ln_eps, ln_rstd = sem("ln_stats"), sem("ln_aggr"), sem("ln_eps"), sem("ln_rstd")
        xn_ready = sem("xn_ready")
        side_ready, side_dve, side_act = sem("side_ready"), sem("side_dve"), sem("side_act")
        q_split_steps, k_split_steps = sem("q_split_steps"), sem("k_split_steps")
        vB_set = sem("vB_set")
        m_split_steps = sem("m_split_steps")
        scores_ready, exp_done, masked = sem("scores_ready"), sem("exp_done"), sem("masked")
        pv_done, o_copied = sem("pv_done"), sem("o_copied")
        ln_sums_ready = sem("ln_sums_ready")
        recip_done, attn_ready = sem("recip_done"), sem("attn_ready")
        z_ready, x1_ready, xn2_ready = sem("z_ready"), sem("x1_ready"), sem("xn2_ready")
        shift_ready, mix_ready = sem("shift_ready"), sem("mix_ready")
        gate_den, gate_ready, k_act_ready = sem("gate_den"), sem("gate_ready"), sem("k_act_ready")
        zf_ready, fin_ready = sem("zf_ready"), sem("fin_ready")

        def upto(kind, e, it, each=1, back=0):
            return each * (plan.n[kind, e] + 1 - back) + each * plan.per[kind] * it

        def in_batch(e, it, per, n):
            return per * e[1] + n + per * it

        def walk(eng, do):
            for e in plan.first:
                do(e, 0)
            for part in plan.laps:
                for e in part:
                    do(e, 0)
            for e in plan.last:
                do(e, 0)

        def batch(e, it):
            return e[1] if isinstance(it, int) and it == 0 else it + e[1]

        def prev(e):
            return (e[0], e[1] - 1) + e[2:]

        def half_cols(h):
            return slice(h * HALF, (h + 1) * HALF)

        def tiles(ap):
            return ap.rearrange("p (t d) -> p t d", d=D)

        def side_bank(e, n=HALF):
            return side_ps[:, plan.bank[e] * HALF:plan.bank[e] * HALF + n]

        def set_of(e):
            return plan.n["set", ("unit", e[1], e[2], set_end(e[3]))]

        everything = [e for part in [plan.first] + plan.laps + [plan.last] for e in part]
        all_sets = [e for e in everything if e[0] == "unit" and last_of_set(e[3])]
        all_closings = [e for e in everything if e[0] == "mT"]

        def split_step(engine, i, src_a, src_b, whole, rest, parts):
            if i == 0:
                return engine.tensor_tensor(out=whole, in0=src_a, in1=src_b, op=ALU.add)
            if i == 1:
                return engine.tensor_copy(parts[0], whole)
            if i == 2:
                return engine.tensor_tensor(out=rest, in0=whole, in1=parts[0], op=ALU.subtract)
            if i == 3:
                return engine.tensor_copy(parts[1], rest)
            return engine.tensor_tensor(out=parts[2], in0=rest, in1=parts[1], op=ALU.subtract)

        def q_split_of(h):
            return (rot_a[:, h, :], rot_b[:, h, :], rot[:, h, :], rot_rest[:, h, :],
                    [q_parts[:, n, half_cols(h)] for n in range(3)])

        k_split_of = (krot_a[:, :], krot_b[:, :], krot[:, :], krot_rest[:, :],
                      [k_parts[:, n, :] for n in range(3)])

        block = ctx.enter_context(nc.Block())

        @block.sync
        def _(sp):
            sp.dma_start(xin[:, :, :], x[0].rearrange("(t p) d -> p t d", p=P)).then_inc(x_loaded, 16)
            sp.dma_start(w[:, :], weights[:, :]).then_inc(w_loaded, 16)
            sp.dma_start(c[:, :], consts[:, :]).then_inc(c_loaded, 16)

            def do(e, it):
                kind = e[0]
                if kind == "x_load" and not (e[1] == 0):
                    sp.wait_ge(xn_ready, upto("x_norm", prev(("x_norm", e[1])), it))
                    sp.dma_start(xin[:, :, :], x[batch(e, it)].rearrange("(t p) d -> p t d", p=P))\
                      .then_inc(x_loaded, 16)
                elif kind == "xres_load":
                    if e[1] > 0:
                        sp.wait_ge(x1_ready, upto("x1", ("x1", e[1] - 1, 1), it))
                    sp.dma_start(xres[:, :, :], x[batch(e, it)].rearrange("(t p) d -> p t d", p=P))\
                      .then_inc(xres_loaded, 16)
                elif kind == "k_store":
                    sp.wait_ge(k_split_steps, upto("k_split", ("k_split", e[1], 4), it))
                    if e[1] > 0:
                        sp.wait_ge(k_max_A_loaded, in_batch(e, it, 96, 0))
                    for h in range(2):
                        sp.dma_start(k_parts_dram[:, :, half_cols(h)].rearrange("c d s -> d c s"),
                                     k_parts[32 * h:32 * h + HD, :, :]).then_inc(k_stored, 16)
                elif kind == "k_max_load":
                    b = e[1]
                    sp.wait_ge(k_stored, upto("k_store", ("k_store", b), it, each=32))
                    if b == 0:
                        sp.wait_ge(k_cleared, 1)
                    else:
                        sp.wait_ge(side_ready, upto("side", ("max", b - 1, 2, len(MAX_JOBS) - 1), it))
                        sp.wait_ge(kB_loaded, in_batch(e, it, 48, 0))
                        sp.wait_ge(k_main_A_loaded, in_batch(e, it, 32, 0))
                    for a in range(2):
                        for row, n in ((0, 3), (3, 2), (5, 1)):
                            sp.dma_start(k_max_A[64 * a + HD * row:64 * a + HD * (row + n), a, :],
                                         k_parts_dram[0:n].rearrange("c d s -> (c d) s"))\
                              .then_inc(k_max_A_loaded, 16)
                elif kind == "k_main_load":
                    b = e[1]
                    if b > 0:
                        sp.wait_ge(scores_ready, upto("unit", ("unit", b - 1, 1, len(UNITS) - 1), it))
                    sp.wait_ge(k_max_A_loaded, in_batch(e, it, 96, 96))
                    for a in range(2):
                        rows = slice(64 * a, 64 * a + KROWS)
                        sp.dma_start(k_main_A[rows, a, :], k_max_A[rows, a, :]).then_inc(k_main_A_loaded, 16)
                elif kind == "kB_load":
                    b = e[1]
                    if b > 0:
                        sp.wait_ge(side_ready, upto("side", ("max", b - 1, 3, len(MAX_JOBS) - 1), it))
                        sp.wait_ge(scores_ready, upto("unit", ("unit", b - 1, 3, len(UNITS) - 1), it))
                    sp.wait_ge(k_max_A_loaded, in_batch(e, it, 96, 96))
                    sp.dma_start(k_max_B[:, :, :], k_max_A[:, :, :]).then_inc(kB_loaded, 16)
                    for a in range(2):
                        rows = slice(64 * a, 64 * a + KROWS)
                        sp.dma_start(k_main_B[rows, a, :], k_max_A[rows, a, :]).then_inc(kB_loaded, 16)
                elif kind == "q_store":
                    b = e[1]
                    sp.wait_ge(q_split_steps, upto("q_split", ("q_split", b, 1, 4), it))
                    if b > 0:
                        for g in range(G):
                            sp.wait_ge(q_loaded[g], in_batch(e, it, 32, 0))
                    for row, part in enumerate(Q_PART):
                        sp.dma_start(q_rows_dram[:, row], q_parts[:, part, :]).then_inc(q_stored, 16)
                elif kind == "q_load":
                    _, b, g = e
                    sp.wait_ge(q_stored, upto("q_store", ("q_store", b), it, each=16 * len(Q_PART)))
                    if b == 0:
                        sp.wait_ge(q_cleared, 1)
                    else:
                        sp.wait_ge(scores_ready, upto("unit", ("unit", b - 1, g, len(UNITS) - 1), it))
                    for a in range(2):
                        sp.dma_start(qs[64 * a:64 * a + KROWS, g, :, :],
                                     q_rows_dram[G * a + g].rearrange("c (d r) s -> (c d) r s", r=2))\
                          .then_inc(q_loaded[g], 16)
                elif kind == "m_load":
                    _, b, g = e
                    sp.wait_ge(side_act, upto("side_act", ("mT", b, g), it))
                    for a in range(2):
                        sp.dma_start(qs[64 * a + KROWS:64 * a + ROWS, g, :, :],
                                     m_rows[48 * a:48 * a + 48, g % 2, :]).then_inc(m_loaded[g % 2], 16)
                elif kind == "o_copy":
                    _, b, g, qh = e
                    sp.wait_ge(o_copied, upto("o_copy", e, it))
                    if b > 0:
                        sp.wait_ge(attn_ready, upto("o_norm", ("o_norm", b - 1, qh), it))
                    for j in range(4):
                        sp.dma_start(att[32 * g + HD * j:32 * g + HD * (j + 1), qh, :, :],
                                     o_out[32 * j:32 * j + 2 * HD, qh, :]).then_inc(o_moved[qh], 16)
                elif kind == "out":
                    _, b, h = e
                    sp.wait_ge(fin_ready, upto("out", e, it))
                    sp.dma_start(out[batch(e, it)].rearrange("(h t p) d -> h p t d", h=2, p=P)[h],
                                 tiles(fin[:, h, :])).then_inc(out_stored[h], 16)

            walk(sp, do)
            for h in range(2):
                sp.wait_ge(out_stored[h], 16 * B)
            sp.wait_ge(q_stored, 16 * len(Q_PART) * B)
            sp.wait_ge(k_stored, 32 * B)

        @block.tensor
        def _(pe):
            pe.wait_ge(w_loaded, 16)
            pe.wait_ge(c_loaded, 16)
            pe.wait_ge(consts_set, 1)

            def take_side(e, it):
                for user in plan.before[e]:
                    if user[0] in ACT_JOBS:
                        pe.wait_ge(side_act, upto("side_act", user, it))
                    else:
                        pe.wait_ge(side_dve, upto("side_dve", user, it))
                return side_bank(e)

            def do(e, it):
                kind = e[0]
                if kind == "unit":
                    _, b, g, i = e
                    qh, kt, heads, width = UNITS[i]
                    u = plan.n["unit", e]
                    if i == 0:
                        pe.wait_ge(m_loaded[g % 2], in_batch(e, it, 64, 32 * (g // 2 + 1)))
                        if g == 0:
                            pe.wait_ge(k_main_A_loaded, in_batch(e, it, 32, 32))
                        if g == 2:
                            pe.wait_ge(kB_loaded, in_batch(e, it, 48, 48))
                    if u >= S_RING:
                        pe.wait_ge(exp_done, upto("unit", e, it, back=S_RING))
                    q0 = (qh + 1) * HALF - width
                    k_main = k_main_A if g < 2 else k_main_B
                    for n, j in enumerate(heads):
                        last = nc.tensor.matmul(
                            score_ps[:, u % S_RING, n * width:(n + 1) * width],
                            k_main[:, j % 2, kt * P:(kt + 1) * P],
                            qs[:, g, j // 2, q0:q0 + width], start=True, stop=True)
                    last.then_inc(scores_ready, 1)
                elif kind == "pv":
                    _, b, g, qh, kt = e
                    end = ("unit", b, g, max(i for i, un in enumerate(UNITS) if un[:2] == (qh, kt)))
                    width = UNITS[end[3]][3]
                    if kt >= 4 * qh:
                        pe.wait_ge(masked, upto("diagonal", end, it))
                    else:
                        pe.wait_ge(exp_done, upto("unit", end, it))
                    if kt == 0:
                        if plan.n["o_copy", ("o_copy", b, g, qh)] >= 1:
                            pe.wait_ge(o_copied, upto("o_copy", ("o_copy", b, g, qh), it, back=1))
                        if qh == 0 and g == 2:
                            pe.wait_ge(vB_set, upto("vB_copy", ("vB_copy", b), it))
                        if qh == 0 and g == 0:
                            pe.wait_ge(side_dve, upto("side_dve", ("v", b, 1), it))
                    v = vA if g < 2 else vB
                    for j in range(4):
                        last = nc.tensor.matmul(
                            out_ps[32 * j:32 * j + VW, HALF - width:HALF], v[:, kt, :],
                            probs[:, set_of(end) % P_RING, j * width:(j + 1) * width],
                            start=kt == 0, stop=kt == 4 * qh + 3)
                    last.then_inc(pv_done, 1)
                elif kind == "max":
                    _, b, g, i = e
                    t, heads = MAX_JOBS[i]
                    n = (t + 1) * P
                    if i == 0:
                        pe.wait_ge(q_loaded[g], in_batch(e, it, 32, 32))
                        if g == 0:
                            pe.wait_ge(k_max_A_loaded, in_batch(e, it, 96, 96))
                        if g == 3:
                            pe.wait_ge(kB_loaded, in_batch(e, it, 48, 48))
                    k_max = k_max_A if g < 3 else k_max_B
                    take_side(e, it)
                    ps = side_bank(e, len(heads) * n)
                    for m, j in enumerate(heads):
                        for k0 in range(0, n, HALF):
                            k1 = min(n, k0 + HALF)
                            last = nc.tensor.matmul(
                                ps[:, m * n + k0:m * n + k1], qs[:, g, j // 2, t * P:(t + 1) * P],
                                k_max[:, j % 2, k0:k1], start=True, stop=True)
                    last.then_inc(side_ready, 1)
                elif kind == "mT":
                    _, b, g = e
                    ps = take_side(e, it)
                    pe.wait_ge(m_split_steps, upto("m_split", ("m_split", b, g, 4), it))
                    nc.tensor.transpose(ps.bitcast(BF16)[0:96, 0:P], m_parts[:, g % 2, :], ident_bf[:, :])\
                      .then_inc(side_ready, 1)
                elif kind == "xT":
                    _, b, h = e
                    ps = take_side(e, it)
                    if h == 0:
                        pe.wait_ge(xn_ready, upto("x_norm", ("x_norm", b), it))
                    for t in range(4):
                        last = nc.tensor.transpose(ps[:, t * P:(t + 1) * P], xn[:, 4 * h + t, :], ident)
                    last.then_inc(side_ready, 1)
                elif kind in ("ka", "kb"):
                    b = e[1]
                    ps = take_side(e, it)
                    pe.wait_ge(side_act, upto("side_act", ("xT", b, 1), it))
                    col = W_KA if kind == "ka" else W_KB
                    for h in range(2):
                        last = nc.tensor.matmul(ps[32 * h:32 * h + 32, :], w[:, col:col + 32],
                                                xnT[:, half_cols(h)], start=True, stop=True)
                    last.then_inc(side_ready, 1)
                elif kind in ("qa", "qb"):
                    _, b, h = e
                    ps = take_side(e, it)
                    col = W_QA if kind == "qa" else W_QB
                    nc.tensor.matmul(ps, w[:, col:col + P], xnT[:, half_cols(h)], start=True, stop=True)\
                      .then_inc(side_ready, 1)
                elif kind == "v":
                    _, b, h = e
                    ps = take_side(e, it)
                    for t in range(4):
                        last = nc.tensor.matmul(ps[:, t * HD:(t + 1) * HD], xnT[:, (4 * h + t) * P:(4 * h + t + 1) * P],
                                                w[:, W_V:W_V + HD], start=True, stop=True)
                    last.then_inc(side_ready, 1)
                elif kind in ("y", "r", "f"):
                    _, b, h = e
                    ps = take_side(e, it)
                    src, col = {"y": (attn, W_O), "r": (xr, W_R), "f": (k_act, W_VF)}[kind]
                    if kind == "y":
                        pe.wait_ge(attn_ready, upto("o_norm", ("o_norm", b, h), it))
                    elif kind == "r":
                        pe.wait_ge(mix_ready, upto("mix", ("mix", b, h), it))
                    else:
                        pe.wait_ge(k_act_ready, upto("sq", ("sq", b, h), it))
                    for t in range(4):
                        last = nc.tensor.matmul(ps[:, t * P:(t + 1) * P], src[:, h, t * P:(t + 1) * P],
                                                w[:, col:col + D], start=True, stop=True)
                    last.then_inc(side_ready, 1)
                elif kind == "nT":
                    _, b, h = e
                    ps = take_side(e, it)
                    pe.wait_ge(xn2_ready, upto("x1_norm", ("x1_norm", b, h), it))
                    for t in range(4):
                        last = nc.tensor.transpose(ps[:, t * P:(t + 1) * P], xn2[:, h, t * P:(t + 1) * P], ident)
                    last.then_inc(side_ready, 1)
                elif kind == "k":
                    _, b, h = e
                    ps = take_side(e, it)
                    nc.tensor.matmul(ps, w[:, W_K:W_K + D], xk[:, h, :], start=True, stop=True)\
                      .then_inc(side_ready, 1)

            walk(pe, do)

        @block.scalar
        def _(act):
            nc.scalar.preload_act_table_set("natural_log_exp_and_others")

            def do(e, it):
                kind = e[0]
                if kind == "unit":
                    _, b, g, i = e
                    qh, kt, heads, width = UNITS[i]
                    u = plan.n["unit", e]
                    if i == 0 or last_of_set(i - 1):
                        mine = set_of(e)
                        if mine >= P_RING:
                            _, ob, og, oi = all_sets[mine - P_RING]
                            act.wait_ge(pv_done, upto("pv", ("pv", ob, og) + UNITS[oi][:2], it))
                    act.wait_ge(scores_ready, upto("unit", e, it))
                    n = len(heads) * width
                    nc.scalar.activation(probs[:, set_of(e) % P_RING, heads[0] * width:heads[0] * width + n],
                                         score_ps[:, u % S_RING, 0:n],
                                         ACT.Exp, scale=SCALE).then_inc(exp_done, 1)
                elif kind == "o_copy":
                    _, b, g, qh = e
                    act.wait_ge(pv_done, upto("pv", ("pv", b, g, qh, 4 * qh + 3), it))
                    if plan.n["o_copy", e] >= 2:
                        act.wait_ge(o_moved[qh], in_batch(e, it, 256, 64 * g))
                    nc.scalar.activation(o_out[:, qh, :], out_ps[:, :], ACT.Copy).then_inc(o_copied, 1)
                elif kind == "o_norm":
                    _, b, h = e
                    act.wait_ge(o_moved[h], in_batch(e, it, 256, 256))
                    nc.scalar.activation(recip[:, h, :], att[:, h, 1, :], ACT.Ln).then_inc(ln_sums_ready, 1)
                    act.wait_ge(ln_sums_ready, upto("o_norm", e, it))
                    nc.scalar.activation(recip[:, h, :], recip[:, h, :], ACT.Exp, scale=-1.0)\
                      .then_inc(recip_done, 1)
                elif kind in ACT_JOBS:
                    ps = side_bank(e)
                    act.wait_ge(side_ready, upto("side", e, it))
                    if kind == "mT":
                        if plan.n["mT", e] >= 2:
                            act.wait_ge(m_loaded[e[2] % 2], in_batch(e, it, 64, 32 * (e[2] // 2)))
                        nc.scalar.activation(m_rows[:, e[2] % 2, :], ps.bitcast(BF16)[0:96, 0:P], ACT.Copy)\
                          .then_inc(side_act, 1)
                        return
                    h = e[2]
                    if kind == "xT":
                        dst, func, scale = xnT[:, half_cols(h)], ACT.Copy, 1.0
                    elif kind == "y":
                        dst, func, scale = y[:, h, :], ACT.Copy, 1.0
                    elif kind == "nT":
                        dst, func, scale = xn2T[:, 1 + h * HALF:1 + (h + 1) * HALF], ACT.Copy, 1.0
                    elif kind == "r":
                        dst, func, scale = e_neg[:, h, :], ACT.Exp, -1.0
                    else:
                        dst, func, scale = k_relu[:, h, :], ACT.Relu, 1.0
                    nc.scalar.activation(dst, ps, func, scale=scale).then_inc(side_act, 1)
                elif kind == "q_split" and e[3] in (1, 3):
                    _, b, h, i = e
                    act.wait_ge(q_split_steps, upto(kind, e, it, back=1))
                    if i == 1 and b > 0:
                        act.wait_ge(q_stored, upto("q_store", ("q_store", b - 1), it, each=96))
                    _, _, whole, rest, parts = q_split_of(h)
                    nc.scalar.activation(parts[i // 2], whole if i == 1 else rest, ACT.Copy)\
                      .then_inc(q_split_steps, 1)
                elif kind == "k_split" and e[2] in (1, 3):
                    _, b, i = e
                    act.wait_ge(k_split_steps, upto(kind, e, it, back=1))
                    if i == 1 and b > 0:
                        act.wait_ge(k_stored, upto("k_store", ("k_store", b - 1), it, each=32))
                    _, _, whole, rest, parts = k_split_of
                    nc.scalar.activation(parts[i // 2], whole if i == 1 else rest, ACT.Copy)\
                      .then_inc(k_split_steps, 1)

            walk(act, do)

        @block.vector
        def _(dve):
            for k in (k_max_A, k_main_A, k_main_B):
                nc.vector.memset(k[:, :, :].bitcast(F32), 0.0).then_inc(k_zero, 1)
            dve.wait_ge(k_zero, 3)
            for k in (k_main_A, k_main_B):
                nc.vector.memset(k[32:64, 0, :], 1.0)
                last = nc.vector.memset(k[96:128, 1, :], 1.0)
            last.then_inc(k_cleared, 1)
            for v in (vA, vB):
                nc.vector.memset(v[:, :, 0:2 * HD].rearrange("p t (d w) -> p t d w", w=2)[:, :, :, 1], 1.0)
                nc.vector.memset(v[:, :, 2 * HD:VW], 0.0)
            nc.vector.memset(xn2T[:, 0:1], 0.0)
            dve.wait_ge(c_loaded, 16)
            nc.vector.tensor_copy(ident_bf[:, :], ident).then_inc(consts_set, 1)
            dve.wait_ge(w_loaded, 16)
            nc.vector.tensor_scalar(one_minus_mu[:, :], w[:, W_MU:W_MU + 2], -1.0, 1.0, ALU.mult, ALU.add)\
              .then_inc(mu_set, 1)
            dve.wait_ge(mu_set, 1)

            def norm_stats(src, n, e, it):
                for t in range(n):
                    last = nc.vector.bn_stats(stats[:, t, :], src[:, t, :])
                last.then_inc(ln_stats, 1)
                dve.wait_ge(ln_stats, upto("ln", e, it))
                for t in range(n):
                    last = nc.vector.bn_aggr(mv[:, t, :], stats[:, t, :])
                last.then_inc(ln_aggr, 1)

            def norm_apply(dst, src, n, e, it, done):
                dve.wait_ge(ln_rstd, upto("ln", e, it))
                for t in range(n):
                    last = nc.vector.tensor_scalar(dst[:, t, :], src[:, t, :], mv[:, t, 0:1], rstd[:, t:t + 1],
                                                   ALU.subtract, ALU.mult)
                last.then_inc(done, 1)

            def do(e, it):
                kind = e[0]
                if kind == "max":
                    _, b, g, i = e
                    t, heads = MAX_JOBS[i]
                    n = (t + 1) * P
                    ps = side_bank(e, len(heads) * n)
                    if i == 0 and plan.n["mT", ("mT", b, g)] >= 2:
                        _, ob, og = all_closings[plan.n["mT", ("mT", b, g)] - 2]
                        dve.wait_ge(m_split_steps, upto("m_split", ("m_split", ob, og, 0), it))
                    dve.wait_ge(side_ready, upto("side", e, it))
                    for m, j in enumerate(heads):
                        col = 16 * (j % 2) + 8 * (j // 2) + t
                        seg = ps[:, m * n:(m + 1) * n]
                        last = nc.vector.tensor_tensor_reduce(
                            out=seg, in0=seg, in1=c[:, C_MASK + S - n:C_MASK + S], scale=1.0,
                            scalar=LOWEST, op0=ALU.add, op1=ALU.max, accum_out=row_max[:, g % 2, col:col + 1])
                    last.then_inc(side_dve, 1)
                elif kind in ("q_split", "k_split") and e[1] == 0 and e[-1] in (0, 2, 4):
                    i = e[-1]
                    done, of = (q_split_steps, q_split_of(e[2])) if kind == "q_split" else (k_split_steps, k_split_of)
                    if i == 0:
                        dve.wait_ge(side_dve, upto("side_dve", ("qb", 0, e[2]) if kind == "q_split" else ("kb", 0), it))
                    else:
                        dve.wait_ge(done, upto(kind, e, it, back=1))
                    split_step(nc.vector, i, *of).then_inc(done, 1)
                elif kind == "x_stats":
                    dve.wait_ge(x_loaded, upto("x_load", ("x_load", e[1]), it, each=16))
                    norm_stats(xin, NT, e, it)
                elif kind == "x_norm":
                    norm_apply(xn, xin, NT, ("x_stats", e[1]), it, xn_ready)
                elif kind in ("qa", "qb"):
                    _, b, h = e
                    dve.wait_ge(side_ready, upto("side", e, it))
                    dst, col = (rot_a, C_COS) if kind == "qa" else (rot_b, C_SIN)
                    nc.vector.tensor_tensor(dst[:, h, :], side_bank(e),
                                            c[:, col + h * HALF:col + (h + 1) * HALF], ALU.mult)\
                      .then_inc(side_dve, 1)
                elif kind in ("ka", "kb"):
                    dve.wait_ge(side_ready, upto("side", e, it))
                    dst, col = (krot_a, C_KCOS) if kind == "ka" else (krot_b, C_KSIN)
                    nc.vector.tensor_tensor(dst[:, :], side_bank(e)[0:64, :],
                                            c[0:64, col:col + HALF], ALU.mult).then_inc(side_dve, 1)
                elif kind == "v":
                    _, b, h = e
                    if h == 0 and b > 0:
                        dve.wait_ge(vB_set, upto("vB_copy", ("vB_copy", b - 1), it))
                        dve.wait_ge(pv_done, upto("pv", ("pv", b - 1, 1, 1, 7), it))
                    dve.wait_ge(side_ready, upto("side", e, it))
                    nc.vector.tensor_copy(vA[:, 4 * h:4 * h + 4, 0:2 * HD:2],
                                          side_bank(e, 4 * HD)
                                          .rearrange("p (t d) -> p t d", d=HD)).then_inc(side_dve, 1)
                elif kind == "o_norm":
                    _, b, h = e
                    dve.wait_ge(recip_done, upto("o_norm", e, it))
                    nc.vector.tensor_tensor(attn[:, h, :], att[:, h, 0, :], recip[:, h, :], ALU.mult)\
                      .then_inc(attn_ready, 1)
                elif kind == "y_stats":
                    dve.wait_ge(side_act, upto("side_act", ("y", e[1], e[2]), it))
                    norm_stats(tiles(y[:, e[2], :]), 4, e, it)
                elif kind == "y_norm":
                    norm_apply(tiles(z[:, e[2], :]), tiles(y[:, e[2], :]), 4, ("y_stats",) + e[1:], it, z_ready)
                elif kind == "x1_stats":
                    dve.wait_ge(x1_ready, upto("x1", ("x1", e[1], e[2]), it))
                    norm_stats(tiles(x1[:, e[2], :]), 4, e, it)
                elif kind == "x1_norm":
                    norm_apply(tiles(xn2[:, e[2], :]), tiles(x1[:, e[2], :]), 4, ("x1_stats",) + e[1:], it,
                               xn2_ready)
                elif kind == "mix":
                    _, b, h = e
                    dve.wait_ge(shift_ready, upto("diff", ("diff", b, h), it))
                    for n, dst in enumerate((xr, xk)):
                        last = nc.vector.scalar_tensor_tensor(
                            out=dst[:, h, :], in0=shift[:, h, :], scalar=one_minus_mu[:, n:n + 1],
                            in1=xn2T[:, 1 + h * HALF:1 + (h + 1) * HALF], op0=ALU.mult, op1=ALU.add)
                    last.then_inc(mix_ready, 1)
                elif kind == "sig":
                    _, b, h = e
                    dve.wait_ge(side_act, upto("side_act", ("r", b, h), it))
                    nc.vector.tensor_scalar_add(e_neg[:, h, :], e_neg[:, h, :], 1.0).then_inc(gate_den, 1)
                    dve.wait_ge(gate_den, upto("sig", e, it))
                    nc.vector.reciprocal(gate[:, h, :], e_neg[:, h, :]).then_inc(gate_ready, 1)
                elif kind == "f":
                    _, b, h = e
                    dve.wait_ge(gate_ready, upto("sig", ("sig", b, h), it))
                    dve.wait_ge(side_ready, upto("side", e, it))
                    nc.vector.tensor_tensor(ff[:, h, :], side_bank(e), gate[:, h, :],
                                            ALU.mult).then_inc(side_dve, 1)
                elif kind == "f_stats":
                    dve.wait_ge(side_dve, upto("side_dve", ("f", e[1], e[2]), it))
                    norm_stats(tiles(ff[:, e[2], :]), 4, e, it)
                elif kind == "f_norm":
                    norm_apply(tiles(zf[:, e[2], :]), tiles(ff[:, e[2], :]), 4, ("f_stats",) + e[1:], it, zf_ready)

            walk(dve, do)

        @block.gpsimd
        def _(pool):
            nc.gpsimd.memset(minus_half[:, :], -0.5)
            nc.gpsimd.memset(qs[:, :, :, :].bitcast(F32), 0.0).then_inc(q_cleared, 1)

            def rstd_of(n, e, it):
                pool.wait_ge(ln_aggr, upto("ln", e, it))
                nc.gpsimd.tensor_scalar(out=var_eps[:, 0:n], in0=mv[:, 0:n, 1], scalar1=EPS, scalar2=None,
                                        op0=ALU.add).then_inc(ln_eps, 1)
                pool.wait_ge(ln_eps, upto("ln", e, it))
                nc.gpsimd.tensor_tensor(out=rstd[:, 0:n], in0=var_eps[:, 0:n], in1=minus_half[:, 0:n],
                                        op=ALU.pow).then_inc(ln_rstd, 1)

            def do(e, it):
                kind = e[0]
                if kind == "unit":
                    _, b, g, i = e
                    qh, kt, heads, width = UNITS[i]
                    if kt < 4 * qh or not last_of_set(i):
                        return
                    pool.wait_ge(exp_done, upto("unit", e, it))
                    d = probs[:, set_of(e) % P_RING, 0:4 * width].rearrange("p (j q) -> p j q", j=4)[:, :, 0:P]
                    nc.gpsimd.affine_select(out=d, in_=d, pattern=[[0, 4], [1, P]], compare_op=ALU.is_ge, fill=0.0,
                                            base=0, channel_multiplier=-1).then_inc(masked, 1)
                elif kind == "q_split" and e[1] > 0 and e[3] in (0, 2, 4):
                    _, b, h, i = e
                    if i == 0:
                        pool.wait_ge(side_dve, upto("side_dve", ("qb", b, h), it))
                    else:
                        pool.wait_ge(q_split_steps, upto(kind, e, it, back=1))
                    split_step(nc.gpsimd, i, *q_split_of(h)).then_inc(q_split_steps, 1)
                elif kind == "k_split" and e[1] > 0 and e[2] in (0, 2, 4):
                    _, b, i = e
                    if i == 0:
                        pool.wait_ge(side_dve, upto("side_dve", ("kb", b), it))
                    else:
                        pool.wait_ge(k_split_steps, upto(kind, e, it, back=1))
                    split_step(nc.gpsimd, i, *k_split_of).then_inc(k_split_steps, 1)
                elif kind == "m_split":
                    _, b, g, i = e
                    par = g % 2
                    parts = [m_parts[:, par, :].rearrange("p (a n x) -> p a n x", a=2, n=3)[:, :, n, :]
                             for n in range(3)]
                    whole, rest = (m[:, par, :].rearrange("p (a x) -> p a x", a=2) for m in (neg_max, neg_rest))
                    if i == 0:
                        pool.wait_ge(side_dve, upto("side_dve", ("max", b, g, len(MAX_JOBS) - 1), it))
                        if plan.n["mT", ("mT", b, g)] >= 2:
                            pool.wait_ge(side_act, upto("side_act", all_closings[plan.n["mT", ("mT", b, g)] - 2], it))
                        nc.gpsimd.tensor_scalar(out=neg_max[:, par, :], in0=row_max[:, par, :], scalar1=-1.0,
                                                scalar2=None, op0=ALU.mult).then_inc(m_split_steps, 1)
                    else:
                        pool.wait_ge(m_split_steps, upto(kind, e, it, back=1))
                        split_step(nc.gpsimd, i, None, None, whole, rest, parts).then_inc(m_split_steps, 1)
                elif kind == "vB_copy":
                    b = e[1]
                    pool.wait_ge(side_dve, upto("side_dve", ("v", b, 1), it))
                    if b > 0:
                        pool.wait_ge(pv_done, upto("pv", ("pv", b - 1, 3, 1, 7), it))
                    nc.gpsimd.tensor_copy(vB[:, :, 0:2 * HD:2], vA[:, :, 0:2 * HD:2]).then_inc(vB_set, 1)
                elif kind.endswith("_stats"):
                    rstd_of(NT if kind == "x_stats" else 4, e, it)
                elif kind == "x1":
                    _, b, h = e
                    pool.wait_ge(z_ready, upto("y_norm", ("y_norm", b, h), it))
                    pool.wait_ge(xres_loaded, upto("xres_load", ("xres_load", b), it, each=16))
                    nc.gpsimd.tensor_tensor(out=tiles(x1[:, h, :]), in0=tiles(z[:, h, :]),
                                            in1=xres[:, 4 * h:4 * h + 4, :], op=ALU.add).then_inc(x1_ready, 1)
                elif kind == "diff":
                    _, b, h = e
                    pool.wait_ge(side_act, upto("side_act", ("nT", b, h), it))
                    nc.gpsimd.tensor_tensor(out=shift[:, h, :], in0=xn2T[:, h * HALF:(h + 1) * HALF],
                                            in1=xn2T[:, 1 + h * HALF:1 + (h + 1) * HALF], op=ALU.subtract)\
                      .then_inc(shift_ready, 1)
                elif kind == "sq":
                    _, b, h = e
                    pool.wait_ge(side_act, upto("side_act", ("k", b, h), it))
                    nc.gpsimd.tensor_tensor(out=k_act[:, h, :], in0=k_relu[:, h, :], in1=k_relu[:, h, :],
                                            op=ALU.mult).then_inc(k_act_ready, 1)
                elif kind == "out":
                    _, b, h = e
                    pool.wait_ge(zf_ready, upto("f_norm", ("f_norm", b, h), it))
                    if b > 0:
                        pool.wait_ge(out_stored[h], in_batch(e, it, 16, 0))
                    nc.gpsimd.tensor_tensor(out=fin[:, h, :], in0=zf[:, h, :], in1=x1[:, h, :], op=ALU.add)\
                      .then_inc(fin_ready, 1)

            walk(pool, do)



def rotary_order():
    half = HD // 2
    near = [2 * i for i in range(half)] + [2 * i + 1 for i in range(half)]
    far = [2 * i + 1 for i in range(half)] + [2 * i for i in range(half)]
    return near, far


def constant_array():
    half = HD // 2
    freqs = (np.float32(1.0) / np.float32(THETA) ** (np.arange(0, HD, 2, dtype=np.float32) / np.float32(HD)))
    ang = np.arange(S, dtype=np.float32)[:, None] * freqs.astype(np.float32)[None, :]
    cos, sin = np.cos(ang).astype(np.float32), np.sin(ang).astype(np.float32)
    cos8 = np.concatenate([cos, cos], axis=1).T
    sin8 = np.concatenate([-sin, sin], axis=1).T
    c = np.zeros((P, C_COLS), np.float32)
    c[:, C_ID:C_ID + P] = np.eye(P, dtype=np.float32)
    c[:, C_MASK + S - P:C_MASK + S] = np.where(np.arange(P)[None, :] > np.arange(P)[:, None], NEG, 0.0)
    for h in range(2):
        c[32 * h:32 * h + HD, C_KCOS:C_KCOS + HALF] = cos8[:, h * HALF:(h + 1) * HALF]
        c[32 * h:32 * h + HD, C_KSIN:C_KSIN + HALF] = sin8[:, h * HALF:(h + 1) * HALF]
    c[:, C_COS:C_COS + S] = np.tile(np.repeat(cos8, 2, axis=0), (P // (2 * HD), 1))
    c[:, C_SIN:C_SIN + S] = np.tile(np.repeat(sin8, 2, axis=0), (P // (2 * HD), 1))
    return c


def weight_array(wq, wk, wv, wo, w_r, w_k, w_v, mu_r, mu_k):
    near, far = rotary_order()
    w = np.zeros((P, W_COLS), np.float32)
    for col, order in ((W_QA, near), (W_QB, far)):
        rows = [HD * (4 * g + 2 * r + a) + d for a in range(2) for g in range(G) for d in order for r in range(2)]
        w[:, col:col + P] = wq[rows, :].T
    w[:, W_KA:W_KA + HD] = wk[:, near]
    w[:, W_KB:W_KB + HD] = wk[:, far]
    w[:, W_V:W_V + HD] = wv
    w[:, W_O:W_O + D] = wo.T
    w[:, W_R:W_R + D] = w_r.T
    w[:, W_K:W_K + D] = w_k.T
    w[:, W_VF:W_VF + D] = w_v.T
    w[:, W_MU] = mu_r
    w[:, W_MU + 1] = mu_k
    return w


def kernel(L0_attn_x, L0_attn_wq, L0_attn_wk, L0_attn_wv, L0_attn_wo, L0_ffn_W_r, L0_ffn_W_k,
           L0_ffn_W_v, L0_ffn_mu_r, L0_ffn_mu_k):
    import concourse.bacc as bacc
    from concourse.bass_utils import run_bass_kernel_spmd

    a = np.asarray
    arrays = {
        "x": np.ascontiguousarray(a(L0_attn_x)),
        "weights": weight_array(a(L0_attn_wq), a(L0_attn_wk), a(L0_attn_wv), a(L0_attn_wo), a(L0_ffn_W_r),
                                a(L0_ffn_W_k), a(L0_ffn_W_v), a(L0_ffn_mu_r), a(L0_ffn_mu_k)),
        "consts": constant_array(),
    }
    nc = bacc.Bacc("TRN2", target_bir_lowering=False, num_devices=1)
    ins = {n: nc.dram_tensor(n, v.shape, F32, kind="ExternalInput").ap() for n, v in arrays.items()}
    out = nc.dram_tensor("out", (B, S, D), F32, kind="ExternalOutput").ap()
    q_dram = nc.dram_tensor("q_rows_dram", (2 * G, len(Q_PART), 2 * HD, S), BF16, kind="Internal").ap()
    k_dram = nc.dram_tensor("k_parts_dram", (3, HD, S), BF16, kind="Internal").ap()
    layer(nc, ins["x"], ins["weights"], ins["consts"], out, q_dram, k_dram)
    result = run_bass_kernel_spmd(nc, [arrays], core_ids=[0])
    return result.results[0]["out"]
```

```python
from contextlib import ExitStack

import numpy as np

import concourse.bass as bass
from concourse import mybir

F32 = mybir.dt.float32
BF16 = mybir.dt.bfloat16
ALU = mybir.AluOpType
ACT = mybir.ActivationFunctionType

P = 128
B, S, D = 4, 1024, 128
H, HD = 16, 8
THETA = 1000.0
EPS = 1e-5
NT = S // P
HALF = S // 2
G = H // 4
SCALE = 1.0 / float(np.sqrt(HD))
NEG = -1e30
LOWEST = -3e38
Q_PART = (0, 0, 0, 1, 1, 2)
KROWS = 8 * len(Q_PART)
ROWS = KROWS + 3
VW = 32
P_RING = 4
S_RING = 3
SIDE_BANKS = 4
LAG = 7
EVAC_LAG = 1

W_QA, W_QB, W_KA, W_KB, W_V = 0, 128, 256, 288, 320
W_O, W_R, W_K, W_VF, W_MU = 328, 456, 584, 712, 840
W_COLS = 842
C_ID, C_MASK, C_KCOS, C_KSIN, C_COS, C_SIN = 0, 128, 1152, 1664, 2176, 3200
C_COLS = 4224



def main_units():
    out = []
    for qh in range(2):
        for kt in range(4 * (qh + 1)):
            width = HALF - P * max(0, kt - 4 * qh)
            n = max(1, min(4, HALF // width)) if width != 384 else 1
            out += [(qh, kt, tuple(range(j, j + n)), width) for j in range(0, 4, n)]
    return out


UNITS = main_units()


def max_jobs():
    out = []
    for t in range(NT):
        n = (4, 2, 1, 1)[t] if t < 4 else 1
        out += [(t, tuple(range(j, j + n))) for j in range(0, 4, n)]
    return out


MAX_JOBS = max_jobs()

ACT_JOBS = ("xT", "mT", "y", "nT", "r", "k")
DVE_JOBS = ("max", "qa", "qb", "ka", "kb", "v", "f")


def last_of_set(i):
    return i + 1 == len(UNITS) or UNITS[i + 1][:2] != UNITS[i][:2]


def set_end(i):
    while not last_of_set(i):
        i += 1
    return i


SECOND_HALF = min(i for i, un in enumerate(UNITS) if un[0] == 1)
MAX_END = (max(i for i, job in enumerate(MAX_JOBS) if job[0] < 4), len(MAX_JOBS) - 1)


def pieces(b):
    return [(0, 4), (4, 8)] if b < B - 1 else LAST_PIECES


LAST_PIECES = [(0, 4), (4, 6), (6, 8)]


POST_BEFORE_GATE = ("o_norm", "o_mul", "y", "y_stats", "y_rstd", "y_norm", "x1", "x1_stats", "x1_rstd", "x1_norm",
                    "nT", "diff", "mix", "r", "k", "den", "sq")
POST_AFTER_GATE = ("f", "f_stats", "f_rstd", "f_norm", "out")
POST_KINDS = POST_BEFORE_GATE + POST_AFTER_GATE


def on_dve(e):
    return e[1] == B - 1 and e[0] in ("y_norm", "x1", "x1_norm", "diff", "sq", "f_norm", "out")


def half_of(b, p):
    return pieces(b)[p][0] // 4


def streams(b):
    def maxima(g):
        return [("max", b, g, i) for i in range(len(MAX_JOBS))]

    def closing(g):
        return [e for h in range(2) for e in
                [("m_split", b, g, h, i) for i in range(5)] + [("mT", b, g, h), ("m_load", b, g, h)]]

    def main(g):
        out, pending = [], []
        for i in range(len(UNITS)):
            out.append(("unit", b, g, i))
            qh, kt = UNITS[i][:2]
            if last_of_set(i):
                pending.append((i + LAG, ("pv", b, g, qh, kt)))
                if kt == 4 * qh + 3:
                    pending.append((i + LAG + EVAC_LAG, ("o_copy", b, g, qh)))
            while pending and pending[0][0] <= i:
                out.append(pending.pop(0)[1])
        return out, [e for _, e in pending]

    mains = []
    carried = []
    for g in range(G):
        group, rest = main(g)
        for i in range(len(carried)):
            group.insert(2 + 3 * i, carried[i])
        carried = rest
        mains.append(group)
    return {
        "close": [e for g in range(G) for e in closing(g)],
        "x": [("x_load", b)] + [(kind, b, h) for kind in ("x_stats", "x_rstd") for h in range(2)]
             + [("prepare", 0)] * (b == 0)
             + [("x_norm", b, 0), ("x_norm", b, 1), ("xT", b, 0), ("xT", b, 1), ("ka", b), ("kb", b), ("qa", b, 0),
                ("qb", b, 0), ("qa", b, 1), ("qb", b, 1), ("v", b, 0), ("v", b, 1)],
        "k": [("k_split", b, i) for i in range(5)] + [("k_store", b), ("k_max_load", b)],
        "q": [("q_split", b, h, i) for h in range(2) for i in range(5)],
        "moves": [[("q_store", b, 0)], [("q_load", b, 0, 0)], [("q_store", b, 1)], [("q_load", b, 0, 1)],
                  [("k_main_load", b)]]
                 + [[("q_load", b, g, h)] for g in range(1, G) for h in range(2)]
                 + [[("kB_load", b)], [("vB_copy", b)], [("xres_load", b)]],
        "post": [[(kind, b, p) for kind in POST_BEFORE_GATE]
                 + [("sig", b, p, i) for i in range(pieces(b)[p][1] - pieces(b)[p][0])]
                 + [(kind, b, p) for kind in POST_AFTER_GATE] for p in range(len(pieces(b)))],
        "max": [maxima(g) for g in range(G)],
        "main": mains, "main rest": carried,
    }


def needs(e):
    kind, b = e[0], e[1]
    if kind == "unit":
        g, i = e[2:]
        if i > 0:
            return [("m_load", b, g, 1)] if i == SECOND_HALF else []
        return [("m_load", b, g, 0)] + [("k_main_load", b)] * (g == 0) + [("kB_load", b)] * (g == 2)
    if kind == "pv":
        _, _, g, qh, kt = e
        last = max(i for i, un in enumerate(UNITS) if un[:2] == (qh, kt))
        return [("unit", b, g, last)] + [("vB_copy", b)] * (g == 2) + [("v", b, 1)] * (g == 0)
    if kind == "o_copy":
        _, _, g, qh = e
        return [("pv", b, g, qh, 4 * qh + 3), ("o_mul", b - 1, qh)]
    if kind == "max":
        g, i = e[2:]
        before = earlier_group(b, g, 2)
        if i > 0:
            return [("m_split",) + before + (1, 0), ("q_load", b, g, 1)] if i == MAX_END[0] + 1 else []
        return [("q_load", b, g, 0), ("m_split",) + before + (0, 0)] + [("k_max_load", b)] * (g == 0) \
            + [("kB_load", b)] * (g == 3)
    if kind == "m_split":
        g, h, i = e[2:]
        return [("m_split", b, g, h, i - 1)] if i else [("max", b, g, MAX_END[h])]
    if kind == "m_load":
        return [("mT",) + e[1:]]
    if kind == "mT":
        g, h = e[2:]
        return [("m_split", b, g, h, 4), ("m_load",) + earlier_group(b, g, 2) + (h,)]
    if kind == "k_split":
        return [("k_split", b, e[2] - 1), ("k_store", b - 1)] if e[2] else [("kb", b)]
    if kind == "q_split":
        _, _, h, i = e
        return [("q_split", b, h, i - 1), ("q_store", b - 1, h)] if i else [("qb", b, h)]
    last_max, last_unit = len(MAX_JOBS) - 1, len(UNITS) - 1
    if kind == "q_load":
        _, _, g, h = e
        return [("q_store", b, h), ("unit", b - 1, g, last_unit)]
    def last_tile(e):
        return pieces(b)[e[2]][1] - pieces(b)[e[2]][0] - 1 if kind == "f" else 0

    table = {
        "prepare": [("x_stats", 0, 1)],
        "x_load": [("x_norm", b - 1, 1)], "x_stats": [("x_load", b)], "x_rstd": [("x_stats",) + e[1:]],
        "x_norm": [("x_rstd",) + e[1:]],
        "xT": [("x_norm",) + e[1:]], "ka": [("xT", b, 1)], "kb": [("xT", b, 1)], "qa": [("xT", b, 1)],
        "qb": [("xT", b, 1)],
        "v": [("xT", b, 1), ("vB_copy", b - 1), ("pv", b - 1, 1, 1, 7)],
        "k_store": [("k_split", b, 4)],
        "k_max_load": [("k_store", b), ("max", b - 1, 2, last_max), ("kB_load", b - 1), ("k_main_load", b - 1)],
        "k_main_load": [("k_max_load", b), ("unit", b - 1, 1, last_unit), ("q_load", 0, 0, 1)],
        "kB_load": [("k_max_load", b), ("q_load", 0, 0, 1), ("max", b - 1, 3, last_max), ("unit", b - 1, 3, last_unit)],
        "vB_copy": [("v", b, 1), ("pv", b - 1, 3, 1, 7)],
        "xres_load": [("x1", b - 1, 1), ("unit", b, 1, 0)],
        "q_store": [("q_split", b, e[-1], 4)] + [("q_load", b - 1, g, e[-1]) for g in range(G)],
        "o_norm": [("o_copy", b, 3, half_of(b, e[-1]) if kind == "o_norm" else 0)],
        "o_mul": [("o_norm",) + e[1:]], "y": [("o_mul",) + e[1:]],
        "y_stats": [("y",) + e[1:]], "y_rstd": [("y_stats",) + e[1:]], "y_norm": [("y_rstd",) + e[1:]],
        "x1": [("y_norm",) + e[1:], ("xres_load", b)], "x1_stats": [("x1",) + e[1:]],
        "x1_rstd": [("x1_stats",) + e[1:]], "x1_norm": [("x1_rstd",) + e[1:]], "nT": [("x1_norm",) + e[1:]],
        "diff": [("nT", b, h) for h in range(e[-1] + 1)], "mix": [("diff",) + e[1:]], "r": [("mix",) + e[1:]],
        "k": [("mix",) + e[1:]], "sq": [("k",) + e[1:]], "den": [("r",) + e[1:]], "sig": [("den",) + e[1:3]],
        "f": [("sq",) + e[1:], ("sig",) + e[1:] + (last_tile(e),)], "f_stats": [("f",) + e[1:]],
        "f_rstd": [("f_stats",) + e[1:]], "f_norm": [("f_rstd",) + e[1:]],
        "out": [("f_norm",) + e[1:]],
    }
    return table[kind]


def earlier_group(b, g, by):
    n = G * b + g - by
    return (n // G, n % G)


def steps(e):
    kind, b = e[0], e[1]
    if kind == "unit":
        qh, kt, heads, width = UNITS[e[3]]
        n = len(heads) * width
        mask = [("pool", 600)] if last_of_set(e[3]) and kt >= 4 * qh else []
        return [("pe", n / 2.4), ("act", 50 + n / 1.2)] + mask
    if kind == "pv":
        width = HALF - P * max(0, e[4] - 4 * e[3])
        return [("pe", 90 + 4 * width / 2.4)]
    if kind == "max":
        t, heads = MAX_JOBS[e[3]]
        n = (t + 1) * P
        return [("pe", len(heads) * n / 2.4), ("dve", len(heads) * (80 + 1.04 * n))]
    if kind in ("k_split", "q_split"):
        if e[-1] in (1, 3):
            return [("act", 480)]
        return [("dve", 600)] if b == 0 else [("pool", 1250)]
    share = 1.0
    if len(e) > 2 and kind in POST_KINDS:
        t0, t1 = pieces(b)[e[2]]
        share = (t1 - t0) / 4
    costs = [(engine, cost * share) for engine, cost in STEPS[kind]]
    if on_dve(e):
        costs = [("dve", (1100 if kind.endswith("_norm") else 600) * share)] + costs[1:]
    return costs


RSTD = [("pool", 1700)]
STEPS = {
    "x_rstd": RSTD, "y_rstd": RSTD, "x1_rstd": RSTD, "f_rstd": RSTD,
    "o_copy": [("act", 480), ("sp", 2500), (None, 2000)], "m_split": [("pool", 180)],
    "mT": [("pe", 60), ("act", 150)], "m_load": [("sp", 1100), (None, 2000)],
    "x_load": [("act", 100), (None, 3500)], "xres_load": [("sp", 450), (None, 3500)],
    "x_stats": [("dve", 1300)], "y_stats": [("dve", 1300)],
    "x1_stats": [("dve", 1300)], "f_stats": [("dve", 1300)],
    "x_norm": [("act", 1600)], "y_norm": [("act", 1600)], "x1_norm": [("act", 1600)],
    "f_norm": [("act", 1600)], "xT": [("pe", 900), ("act", 480)], "nT": [("pe", 900), ("act", 480)],
    "y": [("pe", 900), ("act", 480)], "r": [("pe", 900), ("act", 480)], "k": [("pe", 900), ("act", 480)],
    "ka": [("pe", 930), ("dve", 600)], "kb": [("pe", 930), ("dve", 600)], "qa": [("pe", 900), ("dve", 600)],
    "qb": [("pe", 900), ("dve", 600)], "v": [("pe", 150), ("dve", 100)],
    "f": [("pe", 900), ("dve", 600)], "k_store": [("sp", 1100), (None, 2000)],
    "k_max_load": [("sp", 3600), (None, 2000)], "k_main_load": [("sp", 1200), (None, 2000)],
    "kB_load": [("sp", 2000), (None, 2000)], "q_store": [("sp", 1900), (None, 2000)], "prepare": [("dve", 9000)],
    "q_load": [("sp", 1200), (None, 2000)], "vB_copy": [("pool", 500)],
    "o_norm": [("act", 1000)], "o_mul": [("dve", 600)], "x1": [("pool", 1250)], "diff": [("pool", 1250)],
    "mix": [("dve", 1200)], "sq": [("pool", 1250)], "den": [("dve", 350)], "sig": [("dve", 900)],
    "out": [("pool", 1250), ("sp", 450)],
}


HOP = {"pe": 200, "act": 190, "dve": 150, "pool": 80, "sp": 80, None: 80}


class Planner:

    def __init__(self):
        self.free = {n: 0.0 for n in ("pe", "act", "dve", "pool", "sp")}
        self.done = {}
        self.bank_free = [0.0] * SIDE_BANKS
        self.at_bank = 0
        self.scores_free = [0.0] * S_RING
        self.units = 0
        self.sets, self.out_free = [], 0.0
        self.stats = []

    def bank_of(self, e):
        wide = is_wide(e)
        first = (self.at_bank + 1) // 2 * 2 % SIDE_BANKS if wide else self.at_bank
        return range(first, first + 1 + wide)

    def ready(self, e):
        t = 0.0
        for n in needs(e):
            if n[1] < 0:
                continue
            if n not in self.done:
                return None
            t = max(t, self.done[n])
        if e[0].endswith("_stats") and len(self.stats) >= 2:
            old = self.stats[-2]
            norm = (old[0][:-6] + "_norm",) + old[1:]
            if norm not in self.done:
                return None
            t = max(t, self.done[norm])
        if e[0] in ACT_JOBS + DVE_JOBS:
            t = max([t] + [self.bank_free[k] for k in self.bank_of(e)])
        if e[0] == "unit":
            t = max(t, self.scores_free[self.units % S_RING])
        if e[0] == "pv" and e[4] == 0:
            t = max(t, self.out_free)
        return t

    def take(self, e):
        t = max([self.ready(e)] + [self.done[n] for n in needs(e) if n in self.done])
        banks = self.bank_of(e) if e[0] in ACT_JOBS + DVE_JOBS else None
        for engine, cost in steps(e):
            if e[0] == "unit" and engine == "act" and len(self.sets) >= P_RING:
                t = max(t, self.sets[-P_RING])
            if engine:
                t = max(t, self.free[engine])
                self.free[engine] = t + cost
            t += cost + HOP[engine]
            if banks is not None and engine in ("act", "dve"):
                for k in banks:
                    self.bank_free[k] = t
                self.at_bank = (banks[-1] + 1) % SIDE_BANKS
            if e[0] == "o_copy" and engine == "act":
                self.out_free = t
            if e[0] == "pv":
                self.sets.append(t)
            if e[0] == "unit" and engine == "act":
                self.scores_free[self.units % S_RING] = t
        if e[0] == "unit":
            self.units += 1
        if e[0].endswith("_stats"):
            self.stats.append(e)
        self.done[e] = t

    def order(self, small, main, maxima, lead, early):
        self.at_bank = 0
        out = []
        small = [list(q) for q in small]
        main, maxima = list(main), list(maxima)
        whole = (max(1, len(main)), max(1, len(maxima)))
        while any(small) or main or maxima:
            now = self.free["pe"]
            soonest = None
            for q in small:
                if q:
                    t = self.ready(q[0])
                    if t is not None and (soonest is None or t < soonest[0]):
                        soonest = (t, 2, q)
                        if t <= now + early:
                            break
            if soonest is None or soonest[0] > now + early:
                long_ones = [(q, len(q) / n) for q, n in ((main, whole[0]), (maxima, whole[1] / lead)) if q]
                long_ones.sort(key=lambda x: -x[1])
                options = []
                for rank, (q, _) in enumerate(long_ones):
                    t = self.ready(q[0])
                    if t is not None:
                        options.append((max(t, now), rank, q))
                if options:
                    best = min(options, key=lambda x: x[:2])
                    if soonest is None or best[0] <= soonest[0]:
                        soonest = best
            assert soonest is not None, [q[0] for q in small + [main, maxima] if q]
            e = soonest[2].pop(0)
            self.take(e)
            out.append(e)
        return out


EARLY = (100, -50, 0)


LEAD = (2, 1.15, 5)


def is_wide(e):
    return e[0] == "max" and MAX_JOBS[e[3]][0] >= 4


CUT_CLOSE = 28
CUT_MAX, CUT_MAIN = 24, 34


def timeline():
    planner = Planner()

    def flat(groups):
        return [e for q in groups for e in q]

    w = [streams(b) for b in range(B)]
    now, nxt = w[0], w[1]
    first = planner.order(
        [now["x"], now["k"], now["q"], now["close"][:CUT_CLOSE]] + now["moves"],
        now["main"][0] + now["main"][1][:CUT_MAIN], now["max"][0] + now["max"][1] + now["max"][2][:CUT_MAX],
        LEAD[0], EARLY[0])
    lap = planner.order(
        [nxt["q"], now["post"][1], now["post"][0],
         nxt["k"], now["close"][CUT_CLOSE:] + nxt["close"][:CUT_CLOSE], nxt["x"]]
        + nxt["moves"],
        now["main"][1][CUT_MAIN:] + flat(now["main"][2:]) + now["main rest"] + nxt["main"][0]
        + nxt["main"][1][:CUT_MAIN],
        now["max"][2][CUT_MAX:] + now["max"][3] + nxt["max"][0] + nxt["max"][1] + nxt["max"][2][:CUT_MAX],
        LEAD[1], EARLY[1])
    laps = [[(e[0], e[1] + b) + e[2:] for e in lap] for b in range(B - 1)]
    for e in laps[-1]:
        planner.done[e] = planner.done[(e[0], e[1] - (B - 2)) + e[2:]]
    planner.stats = [(e[0], e[1] + B - 2) + e[2:] for e in planner.stats if e[1] + B - 2 < B]
    for e in [("x_norm", B - 1, 0), ("x_norm", B - 1, 1)]:
        planner.done.setdefault(e, 0.0)
    now = w[B - 1]
    last = planner.order(
        [now["close"][CUT_CLOSE:]] + now["post"],
        now["main"][1][CUT_MAIN:] + flat(now["main"][2:]) + now["main rest"],
        now["max"][2][CUT_MAX:] + now["max"][3], LEAD[2], EARLY[2])
    return first, laps, last


class Counts:

    def __init__(self):
        first, laps, last = timeline()
        parts = [first] + laps + [last]
        self.entries = [e for part in parts for e in part]
        self.n = {}
        count = {}
        for e in self.entries:
            for kind in self.kinds(e):
                self.n[kind, e] = count.get(kind, 0)
                count[kind] = count.get(kind, 0) + 1
        self.place_side_tiles(parts)

    def place_side_tiles(self, parts):
        self.bank, self.before, owner = {}, {}, {}
        for part in parts:
            at_bank = 0
            for e in part:
                if e[0] not in ACT_JOBS + DVE_JOBS:
                    continue
                wide = is_wide(e)
                if wide:
                    at_bank = (at_bank + 1) // 2 * 2 % SIDE_BANKS
                banks = range(at_bank, at_bank + 1 + wide)
                self.bank[e] = at_bank
                self.before[e] = sorted({owner[k] for k in banks if k in owner}, key=lambda u: self.n["side", u])
                for k in banks:
                    owner[k] = e
                at_bank = (at_bank + 1 + wide) % SIDE_BANKS

    @staticmethod
    def kinds(e):
        k = [] if on_dve(e) else [e[0]]
        if e[0] in ACT_JOBS:
            k += ["side", "side_act"]
        if e[0] in DVE_JOBS:
            k += ["side", "side_dve"]
        if e[0].endswith("_stats"):
            k.append("ln")
        if e[0].endswith("_rstd"):
            k.append("rstd")
        if e[0].endswith("_norm") and e[0] != "o_norm":
            k.append("norm on dve" if on_dve(e) else "norm")
        if on_dve(e):
            k.append(e[0] + " on dve")
        if e[0] == "unit" and last_of_set(e[3]):
            k.append("set")
            if UNITS[e[3]][1] >= 4 * UNITS[e[3]][0]:
                k.append("diagonal")
        return k


def layer(nc, x, weights, consts, out, q_rows_dram, k_parts_dram):
    plan = Counts()
    ctx = ExitStack()
    with ctx:
        def sb(name, shape, dt=F32):
            return ctx.enter_context(nc.sbuf_tensor(name, shape, dt))

        def pb(name, shape, dt=F32):
            return ctx.enter_context(nc.psum_tensor(name, shape, dt))

        def sem(name):
            return ctx.enter_context(nc.semaphore(name))

        w = sb("w", [P, W_COLS])
        c = sb("c", [P, C_COLS])
        ident = c[:, C_ID:C_ID + P]
        ident_bf = sb("ident_bf", [P, P], BF16)
        minus_half = sb("minus_half", [P, 4])
        one_minus_mu = sb("one_minus_mu", [P, 2])
        xin = sb("xin", [P, NT, D])
        xn = sb("xn", [P, NT, D])
        xnT = sb("xnT", [P, S])
        rot_a = sb("rot_a", [P, 2, HALF])
        rot_b = sb("rot_b", [P, 2, HALF])
        rot = sb("rot", [P, 2, HALF])
        rot_rest = sb("rot_rest", [P, 2, HALF])
        q_parts = sb("q_parts", [P, 3, S], BF16)
        krot_a = sb("krot_a", [64, HALF])
        krot_b = sb("krot_b", [64, HALF])
        krot = sb("krot", [64, HALF])
        krot_rest = sb("krot_rest", [64, HALF])
        k_parts = sb("k_parts", [64, 3, HALF], BF16)
        qs = sb("qs", [P, G, 2, 2, HALF], BF16)
        k_max_A = sb("k_max_A", [P, 2, S], BF16)
        k_max_B = sb("k_max_B", [P, 2, S], BF16)
        k_main_A = sb("k_main_A", [P, 2, S], BF16)
        k_main_B = sb("k_main_B", [P, 2, S], BF16)
        vA = sb("vA", [P, NT, VW])
        vB = sb("vB", [P, NT, VW])
        row_max = sb("row_max", [P, 2, 2, 16])
        neg_max = sb("neg_max", [P, 2, 2, 16])
        neg_rest = sb("neg_rest", [P, 2, 2, 16])
        m_parts = sb("m_parts", [P, 2, 2, 48], BF16)
        m_rows = sb("m_rows", [48, 2, 2, P], BF16)
        probs = sb("probs", [P, P_RING, 4 * HALF])
        o_out = sb("o_out", [P, 2, HALF])
        att = sb("att", [P, 2, 2, HALF])
        recip = sb("recip", [P, S])
        attn = sb("attn", [P, S])
        xres = sb("xres", [P, NT, D])
        y = sb("y", [P, S])
        z = y
        x1 = sb("x1", [P, S])
        xn2 = sb("xn2", [P, S])
        xn2T = sb("xn2T", [P, S + 1])
        shift = sb("shift", [P, S])
        xr = sb("xr", [P, S])
        xk = sb("xk", [P, S])
        gate = e_neg = sb("e_neg", [P, S])
        k_act = k_relu = sb("k_relu", [P, S])
        zf = ff = sb("ff", [P, S])
        fin = sb("fin", [P, S])
        stats = sb("stats", [P, 2, 4, 6])
        mv = sb("mv", [P, 2, 4, 2])
        var_eps = sb("var_eps", [P, 2, 4])
        neg_mean = sb("neg_mean", [P, 2, 4])
        rstd = sb("rstd", [P, 2, 4])
        shift_by = sb("shift_by", [P, 2, 4])

        score_ps = pb("score_ps", [P, S_RING, HALF])
        side_ps = pb("side_ps", [P, SIDE_BANKS * HALF])
        out_ps = pb("out_ps", [P, HALF])

        w_loaded, ident_loaded = sem("w_loaded"), sem("ident_loaded")
        tables_loaded, mask_loaded = sem("tables_loaded"), sem("mask_loaded")
        x_loaded, xres_loaded = sem("x_loaded"), sem("xres_loaded")
        q_stored, k_stored = [sem(f"q_stored{h}") for h in range(2)], sem("k_stored")
        q_loaded = [[sem(f"q_loaded{g}_{h}") for h in range(2)] for g in range(G)]
        k_max_A_loaded, k_main_A_loaded = sem("k_max_A_loaded"), sem("k_main_A_loaded")
        kB_loaded = sem("kB_loaded")
        m_loaded = [[sem(f"m_loaded{i}_{h}") for h in range(2)] for i in range(2)]
        o_moved = [sem(f"o_moved{i}") for i in range(2)]
        out_stored = [sem(f"out_stored{i}") for i in range(2)]
        k_zero = sem("k_zero")
        q_cleared, k_cleared = sem("q_cleared"), sem("k_cleared")
        consts_set, mu_set = sem("consts_set"), sem("mu_set")
        ln_stats, ln_aggr, ln_eps, ln_rstd = sem("ln_stats"), sem("ln_aggr"), sem("ln_eps"), sem("ln_rstd")
        ln_neg, ln_ready = sem("ln_neg"), sem("ln_ready")
        normed = [sem("normed"), sem("normed_last")]
        x1_ready = [sem("x1_ready"), sem("x1_ready_last")]
        shift_ready = [sem("shift_ready"), sem("shift_ready_last")]
        k_act_ready = [sem("k_act_ready"), sem("k_act_ready_last")]
        fin_ready = [sem("fin_ready"), sem("fin_ready_last")]
        side_ready, side_dve, side_act = sem("side_ready"), sem("side_dve"), sem("side_act")
        q_split_steps, k_split_steps = sem("q_split_steps"), sem("k_split_steps")
        vB_set = sem("vB_set")
        m_split_steps = sem("m_split_steps")
        scores_ready, exp_done, masked = sem("scores_ready"), sem("exp_done"), sem("masked")
        pv_done, o_copied = sem("pv_done"), sem("o_copied")
        ln_sums_ready = sem("ln_sums_ready")
        recip_done, attn_ready = sem("recip_done"), sem("attn_ready")
        mix_ready = sem("mix_ready")
        gate_den, gate_ready = sem("gate_den"), sem("gate_ready")

        everything = plan.entries

        def upto(kind, e, each=1, back=0):
            return each * (plan.n[kind, e] + 1 - back)

        def upto_moved(e):
            name = "norm" if e[0].endswith("_norm") else e[0]
            return upto(name + " on dve" if on_dve(e) else name, e)

        def in_batch(e, per, n):
            return per * e[1] + n

        def walk(eng, do):
            for e in everything:
                do(e)

        def stats_of(e):
            return (e[0][:-5] + "_stats",) + e[1:]

        def rstd_of(e):
            return (e[0][:-5] + "_rstd",) + e[1:]

        def ln_tiles(e):
            return 4 if e[0][:2] == "x_" else count(e)

        def norm_operands(e):
            h = e[2]
            if e[0] == "x_norm":
                return xin[:, 4 * h:4 * h + 4, :], xn[:, 4 * h:4 * h + 4, :]
            src, dst = {"y_norm": (y, z), "x1_norm": (x1, xn2), "f_norm": (ff, zf)}[e[0]]
            return tiles(src[:, cols(e)]), tiles(dst[:, cols(e)])

        def add_residual(engine, e):
            t0, t1 = pieces(e[1])[e[2]]
            return engine.tensor_tensor(out=tiles(x1[:, cols(e)]), in0=tiles(z[:, cols(e)]), in1=xres[:, t0:t1, :],
                                        op=ALU.add)

        def token_shift(engine, e):
            return engine.tensor_tensor(out=shift[:, cols(e)], in0=xn2T[:, 0:S][:, cols(e)],
                                        in1=xn2T[:, 1:1 + S][:, cols(e)], op=ALU.subtract)

        def square(engine, e):
            return engine.tensor_tensor(out=k_act[:, cols(e)], in0=k_relu[:, cols(e)], in1=k_relu[:, cols(e)],
                                        op=ALU.mult)

        def add_ffn(engine, e):
            return engine.tensor_tensor(out=fin[:, cols(e)], in0=zf[:, cols(e)], in1=x1[:, cols(e)], op=ALU.add)

        all_stats = [e for e in everything if e[0].endswith("_stats")]

        def cols(e):
            t0, t1 = pieces(e[1])[e[2]]
            return slice(t0 * P, t1 * P)

        def in_half(e):
            t0, t1 = pieces(e[1])[e[2]]
            return slice(t0 % 4 * P, (t0 % 4 + t1 - t0) * P)

        def count(e):
            t0, t1 = pieces(e[1])[e[2]]
            return t1 - t0

        def half_cols(h):
            return slice(h * HALF, (h + 1) * HALF)

        def tiles(ap):
            return ap.rearrange("p (t d) -> p t d", d=D)

        def side_bank(e, n=HALF):
            return side_ps[:, plan.bank[e] * HALF:plan.bank[e] * HALF + n]

        def set_of(e):
            return plan.n["set", ("unit", e[1], e[2], set_end(e[3]))]

        all_sets = [e for e in everything if e[0] == "unit" and last_of_set(e[3])]

        def split_step(engine, i, src_a, src_b, whole, rest, parts):
            if i == 0:
                return engine.tensor_tensor(out=whole, in0=src_a, in1=src_b, op=ALU.add)
            if i == 1:
                return engine.tensor_copy(parts[0], whole)
            if i == 2:
                return engine.tensor_tensor(out=rest, in0=whole, in1=parts[0], op=ALU.subtract)
            if i == 3:
                return engine.tensor_copy(parts[1], rest)
            return engine.tensor_tensor(out=parts[2], in0=rest, in1=parts[1], op=ALU.subtract)

        def q_split_of(h):
            return (rot_a[:, h, :], rot_b[:, h, :], rot[:, h, :], rot_rest[:, h, :],
                    [q_parts[:, n, half_cols(h)] for n in range(3)])

        k_split_of = (krot_a[:, :], krot_b[:, :], krot[:, :], krot_rest[:, :],
                      [k_parts[:, n, :] for n in range(3)])

        block = ctx.enter_context(nc.Block())

        @block.sync
        def _(sp):
            sp.dma_start(xin[:, :, :], x[0].rearrange("(t p) d -> p t d", p=P)).then_inc(x_loaded, 16)
            sp.dma_start(ident, consts[:, C_ID:C_ID + P]).then_inc(ident_loaded, 16)
            sp.dma_start(w[:, :], weights[:, :]).then_inc(w_loaded, 16)
            sp.dma_start(c[:, C_KCOS:C_COLS], consts[:, C_KCOS:C_COLS]).then_inc(tables_loaded, 16)
            sp.dma_start(c[:, C_MASK:C_KCOS], consts[:, C_MASK:C_KCOS]).then_inc(mask_loaded, 16)

            def do(e):
                kind = e[0]
                if kind == "xres_load":
                    if e[1] > 0:
                        sp.wait_ge(x1_ready[0], upto("x1", ("x1", e[1] - 1, 1)))
                    sp.dma_start(xres[:, :, :], x[e[1]].rearrange("(t p) d -> p t d", p=P))\
                      .then_inc(xres_loaded, 16)
                elif kind == "k_store":
                    sp.wait_ge(k_split_steps, upto("k_split", ("k_split", e[1], 4)))
                    if e[1] > 0:
                        sp.wait_ge(k_max_A_loaded, in_batch(e, 96, 0))
                    for h in range(2):
                        sp.dma_start(k_parts_dram[:, :, half_cols(h)].rearrange("c d s -> d c s"),
                                     k_parts[32 * h:32 * h + HD, :, :]).then_inc(k_stored, 16)
                elif kind == "k_max_load":
                    b = e[1]
                    sp.wait_ge(k_stored, upto("k_store", ("k_store", b), each=32))
                    if b == 0:
                        sp.wait_ge(k_cleared, 1)
                    else:
                        sp.wait_ge(side_ready, upto("side", ("max", b - 1, 2, len(MAX_JOBS) - 1)))
                        sp.wait_ge(kB_loaded, in_batch(e, 48, 0))
                        sp.wait_ge(k_main_A_loaded, in_batch(e, 32, 0))
                    for a in range(2):
                        for row, n in ((0, 3), (3, 2), (5, 1)):
                            sp.dma_start(k_max_A[64 * a + HD * row:64 * a + HD * (row + n), a, :],
                                         k_parts_dram[0:n].rearrange("c d s -> (c d) s"))\
                              .then_inc(k_max_A_loaded, 16)
                elif kind == "k_main_load":
                    b = e[1]
                    if b > 0:
                        sp.wait_ge(scores_ready, upto("unit", ("unit", b - 1, 1, len(UNITS) - 1)))
                    sp.wait_ge(k_max_A_loaded, in_batch(e, 96, 96))
                    for a in range(2):
                        rows = slice(64 * a, 64 * a + KROWS)
                        sp.dma_start(k_main_A[rows, a, :], k_max_A[rows, a, :]).then_inc(k_main_A_loaded, 16)
                elif kind == "kB_load":
                    b = e[1]
                    if b > 0:
                        sp.wait_ge(side_ready, upto("side", ("max", b - 1, 3, len(MAX_JOBS) - 1)))
                        sp.wait_ge(scores_ready, upto("unit", ("unit", b - 1, 3, len(UNITS) - 1)))
                    sp.wait_ge(k_max_A_loaded, in_batch(e, 96, 96))
                    sp.dma_start(k_max_B[:, :, :], k_max_A[:, :, :]).then_inc(kB_loaded, 16)
                    for a in range(2):
                        rows = slice(64 * a, 64 * a + KROWS)
                        sp.dma_start(k_main_B[rows, a, :], k_max_A[rows, a, :]).then_inc(kB_loaded, 16)
                elif kind == "q_store":
                    _, b, h = e
                    sp.wait_ge(q_split_steps, upto("q_split", ("q_split", b, h, 4)))
                    if b > 0:
                        for g in range(G):
                            sp.wait_ge(q_loaded[g][h], in_batch(e, 32, 0))
                    for row, part, n in ((0, 0, 3), (3, 1, 2), (5, 2, 1)):
                        sp.dma_start(q_rows_dram[h, row:row + n].rearrange("c p s -> p c s"),
                                     q_parts[:, part:part + 1, half_cols(h)].broadcast_to([P, n, HALF]))\
                          .then_inc(q_stored[h], 16)
                elif kind == "q_load":
                    _, b, g, h = e
                    sp.wait_ge(q_stored[h], in_batch(e, 48, 48))
                    if b == 0:
                        sp.wait_ge(q_cleared, 1)
                    else:
                        sp.wait_ge(scores_ready, upto("unit", ("unit", b - 1, g, len(UNITS) - 1)))
                    for a in range(2):
                        sp.dma_start(qs[64 * a:64 * a + KROWS, g, h, :, :],
                                     q_rows_dram[h, :, 16 * (G * a + g):16 * (G * a + g + 1)]
                                     .rearrange("c (d r) s -> c d (r s)", r=2)).then_inc(q_loaded[g][h], 16)
                elif kind == "m_load":
                    _, b, g, h = e
                    sp.wait_ge(side_act, upto("side_act", ("mT", b, g, h)))
                    for a in range(2):
                        sp.dma_start(qs[64 * a + KROWS:64 * a + ROWS, g, h, :, :],
                                     m_rows[24 * a:24 * a + 24, g % 2, h, :]).then_inc(m_loaded[g % 2][h], 16)
                elif kind == "o_copy":
                    _, b, g, qh = e
                    sp.wait_ge(o_copied, upto("o_copy", e))
                    if b > 0:
                        sp.wait_ge(attn_ready, upto("o_mul", ("o_mul", b - 1, qh)))
                    for j in range(4):
                        sp.dma_start(att[32 * g + HD * j:32 * g + HD * (j + 1), qh, :, :],
                                     o_out[32 * j:32 * j + 2 * HD, qh, :]).then_inc(o_moved[qh], 16)
                elif kind == "out":
                    _, b, p = e
                    sp.wait_ge(fin_ready[on_dve(e)], upto_moved(e))
                    t0, t1 = pieces(b)[p]
                    sp.dma_start(out[e[1]].rearrange("(t p) d -> p t d", p=P)[:, t0:t1, :],
                                 tiles(fin[:, cols(e)])).then_inc(out_stored[half_of(b, p)], 16)

            walk(sp, do)
            for h in range(2):
                sp.wait_ge(out_stored[h], 16 * sum(half_of(b, p) == h for b in range(B) for p in range(len(pieces(b)))))
            for h in range(2):
                sp.wait_ge(q_stored[h], 48 * B)
            sp.wait_ge(k_stored, 32 * B)

        @block.tensor
        def _(pe):
            pe.wait_ge(w_loaded, 16)
            pe.wait_ge(ident_loaded, 16)

            def take_side(e):
                for user in plan.before[e]:
                    if user[0] in ACT_JOBS:
                        pe.wait_ge(side_act, upto("side_act", user))
                    else:
                        pe.wait_ge(side_dve, upto("side_dve", user))
                return side_bank(e)

            def do(e):
                kind = e[0]
                if kind == "unit":
                    _, b, g, i = e
                    qh, kt, heads, width = UNITS[i]
                    u = plan.n["unit", e]
                    if i == 0:
                        pe.wait_ge(m_loaded[g % 2][0], in_batch(e, 64, 32 * (g // 2 + 1)))
                        if g == 0:
                            pe.wait_ge(k_main_A_loaded, in_batch(e, 32, 32))
                        if g == 2:
                            pe.wait_ge(kB_loaded, in_batch(e, 48, 48))
                    if i == SECOND_HALF:
                        pe.wait_ge(m_loaded[g % 2][1], in_batch(e, 64, 32 * (g // 2 + 1)))
                    if u >= S_RING:
                        pe.wait_ge(exp_done, upto("unit", e, back=S_RING))
                    k_main = k_main_A if g < 2 else k_main_B
                    for n, j in enumerate(heads):
                        last = nc.tensor.matmul(
                            score_ps[:, u % S_RING, n * width:(n + 1) * width],
                            k_main[:, j % 2, kt * P:(kt + 1) * P],
                            qs[:, g, qh, j // 2, HALF - width:HALF], start=True, stop=True)
                    last.then_inc(scores_ready, 1)
                elif kind == "pv":
                    _, b, g, qh, kt = e
                    end = ("unit", b, g, max(i for i, un in enumerate(UNITS) if un[:2] == (qh, kt)))
                    width = UNITS[end[3]][3]
                    if kt >= 4 * qh:
                        pe.wait_ge(masked, upto("diagonal", end))
                    else:
                        pe.wait_ge(exp_done, upto("unit", end))
                    if kt == 0:
                        if plan.n["o_copy", ("o_copy", b, g, qh)] >= 1:
                            pe.wait_ge(o_copied, upto("o_copy", ("o_copy", b, g, qh), back=1))
                        if qh == 0 and g == 2:
                            pe.wait_ge(vB_set, upto("vB_copy", ("vB_copy", b)))
                        if qh == 0 and g == 0:
                            pe.wait_ge(side_dve, upto("side_dve", ("v", b, 1)))
                    v = vA if g < 2 else vB
                    for j in range(4):
                        last = nc.tensor.matmul(
                            out_ps[32 * j:32 * j + VW, HALF - width:HALF], v[:, kt, :],
                            probs[:, set_of(end) % P_RING, j * width:(j + 1) * width],
                            start=kt == 0, stop=kt == 4 * qh + 3)
                    last.then_inc(pv_done, 1)
                elif kind == "max":
                    _, b, g, i = e
                    t, heads = MAX_JOBS[i]
                    n = (t + 1) * P
                    if i == 0:
                        pe.wait_ge(q_loaded[g][0], in_batch(e, 32, 32))
                        if g == 0:
                            pe.wait_ge(k_max_A_loaded, in_batch(e, 96, 96))
                        if g == 3:
                            pe.wait_ge(kB_loaded, in_batch(e, 48, 48))
                    if i == MAX_END[0] + 1:
                        pe.wait_ge(q_loaded[g][1], in_batch(e, 32, 32))
                    k_max = k_max_A if g < 3 else k_max_B
                    take_side(e)
                    ps = side_bank(e, len(heads) * n)
                    for m, j in enumerate(heads):
                        for k0 in range(0, n, HALF):
                            k1 = min(n, k0 + HALF)
                            last = nc.tensor.matmul(
                                ps[:, m * n + k0:m * n + k1], qs[:, g, t // 4, j // 2, t % 4 * P:(t % 4 + 1) * P],
                                k_max[:, j % 2, k0:k1], start=True, stop=True)
                    last.then_inc(side_ready, 1)
                elif kind == "mT":
                    _, b, g, h = e
                    ps = take_side(e)
                    pe.wait_ge(m_split_steps, upto("m_split", ("m_split", b, g, h, 4)))
                    if b == 0 and g == 0 and h == 0:
                        pe.wait_ge(consts_set, 1)
                    nc.tensor.transpose(ps.bitcast(BF16)[0:48, 0:P], m_parts[:, g % 2, h, :], ident_bf[:, :])\
                      .then_inc(side_ready, 1)
                elif kind == "xT":
                    _, b, h = e
                    ps = take_side(e)
                    pe.wait_ge(normed[0], upto_moved(("x_norm", b, h)))
                    for t in range(4):
                        last = nc.tensor.transpose(ps[:, t * P:(t + 1) * P], xn[:, 4 * h + t, :], ident)
                    last.then_inc(side_ready, 1)
                elif kind in ("ka", "kb"):
                    b = e[1]
                    ps = take_side(e)
                    pe.wait_ge(side_act, upto("side_act", ("xT", b, 1)))
                    col = W_KA if kind == "ka" else W_KB
                    for h in range(2):
                        last = nc.tensor.matmul(ps[32 * h:32 * h + 32, :], w[:, col:col + 32],
                                                xnT[:, half_cols(h)], start=True, stop=True)
                    last.then_inc(side_ready, 1)
                elif kind in ("qa", "qb"):
                    _, b, h = e
                    ps = take_side(e)
                    col = W_QA if kind == "qa" else W_QB
                    nc.tensor.matmul(ps, w[:, col:col + P], xnT[:, half_cols(h)], start=True, stop=True)\
                      .then_inc(side_ready, 1)
                elif kind == "v":
                    _, b, h = e
                    ps = take_side(e)
                    for t in range(4):
                        last = nc.tensor.matmul(ps[:, t * HD:(t + 1) * HD], xnT[:, (4 * h + t) * P:(4 * h + t + 1) * P],
                                                w[:, W_V:W_V + HD], start=True, stop=True)
                    last.then_inc(side_ready, 1)
                elif kind in ("y", "r", "f"):
                    _, b, h = e
                    ps = take_side(e)
                    src, col = {"y": (attn, W_O), "r": (xr, W_R), "f": (k_act, W_VF)}[kind]
                    if kind == "y":
                        pe.wait_ge(attn_ready, upto("o_mul", ("o_mul", b, h)))
                    elif kind == "r":
                        pe.wait_ge(mix_ready, upto("mix", ("mix", b, h)))
                    else:
                        pe.wait_ge(k_act_ready[on_dve(("sq", b, h))], upto_moved(("sq", b, h)))
                    for t in range(count(e)):
                        last = nc.tensor.matmul(ps[:, t * P:(t + 1) * P], src[:, cols(e)][:, t * P:(t + 1) * P],
                                                w[:, col:col + D], start=True, stop=True)
                    last.then_inc(side_ready, 1)
                elif kind == "nT":
                    _, b, h = e
                    ps = take_side(e)
                    pe.wait_ge(normed[on_dve(("x1_norm", b, h))], upto_moved(("x1_norm", b, h)))
                    for t in range(count(e)):
                        last = nc.tensor.transpose(ps[:, t * P:(t + 1) * P], xn2[:, cols(e)][:, t * P:(t + 1) * P],
                                                   ident)
                    last.then_inc(side_ready, 1)
                elif kind == "k":
                    _, b, h = e
                    ps = take_side(e)
                    nc.tensor.matmul(ps[:, 0:count(e) * P], w[:, W_K:W_K + D], xk[:, cols(e)], start=True, stop=True)\
                      .then_inc(side_ready, 1)

            walk(pe, do)

        @block.scalar
        def _(act):
            nc.scalar.preload_act_table_set("natural_log_exp_and_others")

            def do(e):
                kind = e[0]
                if kind == "unit":
                    _, b, g, i = e
                    qh, kt, heads, width = UNITS[i]
                    u = plan.n["unit", e]
                    if i == 0 or last_of_set(i - 1):
                        mine = set_of(e)
                        if mine >= P_RING:
                            _, ob, og, oi = all_sets[mine - P_RING]
                            act.wait_ge(pv_done, upto("pv", ("pv", ob, og) + UNITS[oi][:2]))
                    act.wait_ge(scores_ready, upto("unit", e))
                    n = len(heads) * width
                    nc.scalar.activation(probs[:, set_of(e) % P_RING, heads[0] * width:heads[0] * width + n],
                                         score_ps[:, u % S_RING, 0:n],
                                         ACT.Exp, scale=SCALE).then_inc(exp_done, 1)
                elif kind == "o_copy":
                    _, b, g, qh = e
                    act.wait_ge(pv_done, upto("pv", ("pv", b, g, qh, 4 * qh + 3)))
                    if plan.n["o_copy", e] >= 2:
                        act.wait_ge(o_moved[qh], in_batch(e, 256, 64 * g))
                    nc.scalar.activation(o_out[:, qh, :], out_ps[:, :], ACT.Copy).then_inc(o_copied, 1)
                elif kind == "o_norm":
                    _, b, p = e
                    half = half_of(b, p)
                    act.wait_ge(o_moved[half], in_batch(e, 256, 256))
                    nc.scalar.activation(recip[:, cols(e)], att[:, half, 1, in_half(e)], ACT.Ln)\
                      .then_inc(ln_sums_ready, 1)
                    act.wait_ge(ln_sums_ready, upto("o_norm", e))
                    nc.scalar.activation(recip[:, cols(e)], recip[:, cols(e)], ACT.Exp, scale=-1.0)\
                      .then_inc(recip_done, 1)
                elif kind == "x_load" and e[1] > 0:
                    act.wait_ge(normed[0], upto_moved(("x_norm", e[1] - 1, 1)))
                    act.dma_start(xin[:, :, :], x[e[1]].rearrange("(t p) d -> p t d", p=P))\
                      .then_inc(x_loaded, 16)
                elif kind in ("x_norm", "y_norm", "x1_norm", "f_norm") and not on_dve(e):
                    src, dst = norm_operands(e)
                    act.wait_ge(ln_ready, upto("rstd", rstd_of(e)))
                    s = plan.n["ln", stats_of(e)] % 2
                    for t in range(ln_tiles(e)):
                        last = nc.scalar.activation(dst[:, t, :], src[:, t, :], ACT.Identity,
                                                    bias=shift_by[:, s, t:t + 1], scale=rstd[:, s, t:t + 1])
                    last.then_inc(normed[0], 1)
                elif kind in ACT_JOBS:
                    ps = side_bank(e)
                    act.wait_ge(side_ready, upto("side", e))
                    if kind == "mT":
                        _, b, g, h = e
                        if plan.n["mT", e] >= 4:
                            act.wait_ge(m_loaded[g % 2][h], in_batch(e, 64, 32 * (g // 2)))
                        nc.scalar.activation(m_rows[:, g % 2, h, :], ps.bitcast(BF16)[0:48, 0:P], ACT.Copy)\
                          .then_inc(side_act, 1)
                        return
                    h = e[2]
                    if kind == "xT":
                        dst, func, scale = xnT[:, half_cols(h)], ACT.Copy, 1.0
                    elif kind == "y":
                        dst, func, scale = y[:, cols(e)], ACT.Copy, 1.0
                    elif kind == "nT":
                        dst, func, scale = xn2T[:, 1:1 + S][:, cols(e)], ACT.Copy, 1.0
                    elif kind == "r":
                        dst, func, scale = e_neg[:, cols(e)], ACT.Exp, -1.0
                    else:
                        dst, func, scale = k_relu[:, cols(e)], ACT.Relu, 1.0
                    n = HALF if kind == "xT" else count(e) * P
                    nc.scalar.activation(dst, ps[:, 0:n], func, scale=scale).then_inc(side_act, 1)
                elif kind == "q_split" and e[3] in (1, 3):
                    _, b, h, i = e
                    act.wait_ge(q_split_steps, upto(kind, e, back=1))
                    if i == 1 and b > 0:
                        act.wait_ge(q_stored[h], in_batch(e, 48, 0))
                    _, _, whole, rest, parts = q_split_of(h)
                    nc.scalar.activation(parts[i // 2], whole if i == 1 else rest, ACT.Copy)\
                      .then_inc(q_split_steps, 1)
                elif kind == "k_split" and e[2] in (1, 3):
                    _, b, i = e
                    act.wait_ge(k_split_steps, upto(kind, e, back=1))
                    if i == 1 and b > 0:
                        act.wait_ge(k_stored, upto("k_store", ("k_store", b - 1), each=32))
                    _, _, whole, rest, parts = k_split_of
                    nc.scalar.activation(parts[i // 2], whole if i == 1 else rest, ACT.Copy)\
                      .then_inc(k_split_steps, 1)

            walk(act, do)

        @block.vector
        def _(dve):
            def norm_stats(src, tile_count, e):
                n = plan.n["ln", e]
                s = n % 2
                if n >= 2:
                    old = all_stats[n - 2]
                    norm = (old[0][:-6] + "_norm",) + old[1:]
                    dve.wait_ge(normed[on_dve(norm)], upto_moved(norm))
                for t in range(tile_count):
                    last = nc.vector.bn_stats(stats[:, s, t, :], src[:, t, :])
                last.then_inc(ln_stats, 1)
                dve.wait_ge(ln_stats, upto("ln", e))
                for t in range(tile_count):
                    last = nc.vector.bn_aggr(mv[:, s, t, :], stats[:, s, t, :])
                last.then_inc(ln_aggr, 1)

            def do(e):
                kind = e[0]
                if kind == "max":
                    _, b, g, i = e
                    t, heads = MAX_JOBS[i]
                    n = (t + 1) * P
                    ps = side_bank(e, len(heads) * n)
                    h = t // 4
                    if i in (0, MAX_END[0] + 1) and G * b + g >= 2:
                        dve.wait_ge(m_split_steps, upto("m_split", ("m_split",) + earlier_group(b, g, 2) + (h, 0)))
                    dve.wait_ge(side_ready, upto("side", e))
                    for m, j in enumerate(heads):
                        col = 8 * (j % 2) + 4 * (j // 2) + t % 4
                        seg = ps[:, m * n:(m + 1) * n]
                        last = nc.vector.tensor_tensor_reduce(
                            out=seg, in0=seg, in1=c[:, C_MASK + S - n:C_MASK + S], scale=1.0,
                            scalar=LOWEST, op0=ALU.add, op1=ALU.max, accum_out=row_max[:, g % 2, h, col:col + 1])
                    last.then_inc(side_dve, 1)
                elif kind in ("q_split", "k_split") and e[1] == 0 and e[-1] in (0, 2, 4):
                    i = e[-1]
                    done, of = (q_split_steps, q_split_of(e[2])) if kind == "q_split" else (k_split_steps, k_split_of)
                    if i == 0:
                        dve.wait_ge(side_dve, upto("side_dve", ("qb", 0, e[2]) if kind == "q_split" else ("kb", 0)))
                    else:
                        dve.wait_ge(done, upto(kind, e, back=1))
                    split_step(nc.vector, i, *of).then_inc(done, 1)
                elif kind == "x_stats":
                    dve.wait_ge(x_loaded, upto("x_load", ("x_load", e[1]), each=16))
                    norm_stats(xin[:, 4 * e[2]:4 * e[2] + 4, :], 4, e)
                elif kind == "prepare":
                    for k in (k_max_A, k_main_A, k_main_B):
                        nc.vector.memset(k[:, :, :].bitcast(F32), 0.0).then_inc(k_zero, 1)
                    dve.wait_ge(k_zero, 3)
                    for k in (k_main_A, k_main_B):
                        nc.vector.memset(k[32:64, 0, :], 1.0)
                        last = nc.vector.memset(k[96:128, 1, :], 1.0)
                    last.then_inc(k_cleared, 1)
                    for v in (vA, vB):
                        nc.vector.memset(v[:, :, 0:2 * HD].rearrange("p t (d w) -> p t d w", w=2)[:, :, :, 1], 1.0)
                        nc.vector.memset(v[:, :, 2 * HD:VW], 0.0)
                    nc.vector.memset(xn2T[:, 0:1], 0.0)
                    dve.wait_ge(ident_loaded, 16)
                    nc.vector.tensor_copy(ident_bf[:, :], ident).then_inc(consts_set, 1)
                    dve.wait_ge(w_loaded, 16)
                    nc.vector.tensor_scalar(one_minus_mu[:, :], w[:, W_MU:W_MU + 2], -1.0, 1.0, ALU.mult, ALU.add)\
                      .then_inc(mu_set, 1)
                    dve.wait_ge(mu_set, 1)
                    dve.wait_ge(tables_loaded, 16)
                    dve.wait_ge(mask_loaded, 16)
                elif kind in ("qa", "qb"):
                    _, b, h = e
                    dve.wait_ge(side_ready, upto("side", e))
                    dst, col = (rot_a, C_COS) if kind == "qa" else (rot_b, C_SIN)
                    nc.vector.tensor_tensor(dst[:, h, :], side_bank(e),
                                            c[:, col + h * HALF:col + (h + 1) * HALF], ALU.mult)\
                      .then_inc(side_dve, 1)
                elif kind in ("ka", "kb"):
                    dve.wait_ge(side_ready, upto("side", e))
                    dst, col = (krot_a, C_KCOS) if kind == "ka" else (krot_b, C_KSIN)
                    nc.vector.tensor_tensor(dst[:, :], side_bank(e)[0:64, :],
                                            c[0:64, col:col + HALF], ALU.mult).then_inc(side_dve, 1)
                elif kind == "v":
                    _, b, h = e
                    if h == 0 and b > 0:
                        dve.wait_ge(vB_set, upto("vB_copy", ("vB_copy", b - 1)))
                        dve.wait_ge(pv_done, upto("pv", ("pv", b - 1, 1, 1, 7)))
                    dve.wait_ge(side_ready, upto("side", e))
                    nc.vector.tensor_copy(vA[:, 4 * h:4 * h + 4, 0:2 * HD:2],
                                          side_bank(e, 4 * HD)
                                          .rearrange("p (t d) -> p t d", d=HD)).then_inc(side_dve, 1)
                elif kind == "o_mul":
                    _, b, p = e
                    dve.wait_ge(recip_done, upto("o_norm", ("o_norm", b, p)))
                    nc.vector.tensor_tensor(attn[:, cols(e)], att[:, half_of(b, p), 0, in_half(e)],
                                            recip[:, cols(e)], ALU.mult)\
                      .then_inc(attn_ready, 1)
                elif kind == "y_stats":
                    dve.wait_ge(side_act, upto("side_act", ("y", e[1], e[2])))
                    norm_stats(tiles(y[:, cols(e)]), count(e), e)
                elif kind == "x1_stats":
                    x1_done = ("x1", e[1], e[2])
                    dve.wait_ge(x1_ready[on_dve(x1_done)], upto_moved(x1_done))
                    norm_stats(tiles(x1[:, cols(e)]), count(e), e)
                elif kind in ("y_norm", "x1_norm", "f_norm") and on_dve(e):
                    src, dst = norm_operands(e)
                    dve.wait_ge(ln_rstd, upto("rstd", rstd_of(e)))
                    s = plan.n["ln", stats_of(e)] % 2
                    for t in range(ln_tiles(e)):
                        last = nc.vector.tensor_scalar(dst[:, t, :], src[:, t, :], mv[:, s, t, 0:1],
                                                       rstd[:, s, t:t + 1], ALU.subtract, ALU.mult)
                    last.then_inc(normed[1], 1)
                elif kind == "x1" and on_dve(e):
                    dve.wait_ge(normed[1], upto_moved(("y_norm",) + e[1:]))
                    dve.wait_ge(xres_loaded, upto("xres_load", ("xres_load", e[1]), each=16))
                    add_residual(nc.vector, e).then_inc(x1_ready[1], 1)
                elif kind == "diff" and on_dve(e):
                    dve.wait_ge(side_act, upto("side_act", ("nT",) + e[1:]))
                    token_shift(nc.vector, e).then_inc(shift_ready[1], 1)
                elif kind == "sq" and on_dve(e):
                    dve.wait_ge(side_act, upto("side_act", ("k",) + e[1:]))
                    square(nc.vector, e).then_inc(k_act_ready[1], 1)
                elif kind == "out" and on_dve(e):
                    dve.wait_ge(normed[1], upto_moved(("f_norm",) + e[1:]))
                    dve.wait_ge(out_stored[half_of(e[1], e[2])], in_batch(e, 16, 0))
                    add_ffn(nc.vector, e).then_inc(fin_ready[1], 1)
                elif kind == "mix":
                    _, b, h = e
                    dve.wait_ge(shift_ready[on_dve(("diff", b, h))], upto_moved(("diff", b, h)))
                    for n, dst in enumerate((xr, xk)):
                        last = nc.vector.scalar_tensor_tensor(
                            out=dst[:, cols(e)], in0=shift[:, cols(e)], scalar=one_minus_mu[:, n:n + 1],
                            in1=xn2T[:, 1:1 + S][:, cols(e)], op0=ALU.mult, op1=ALU.add)
                    last.then_inc(mix_ready, 1)
                elif kind == "den":
                    _, b, h = e
                    dve.wait_ge(side_act, upto("side_act", ("r", b, h)))
                    nc.vector.tensor_scalar_add(e_neg[:, cols(e)], e_neg[:, cols(e)], 1.0).then_inc(gate_den, 1)
                elif kind == "sig":
                    _, b, h, i = e
                    dve.wait_ge(gate_den, upto("den", ("den", b, h)))
                    tile = slice(i * P, (i + 1) * P)
                    nc.vector.reciprocal(gate[:, cols(e)][:, tile], e_neg[:, cols(e)][:, tile])\
                      .then_inc(gate_ready, 1)
                elif kind == "f":
                    _, b, h = e
                    dve.wait_ge(gate_ready, upto("sig", ("sig", b, h, count(e) - 1)))
                    dve.wait_ge(side_ready, upto("side", e))
                    nc.vector.tensor_tensor(ff[:, cols(e)], side_bank(e, count(e) * P), gate[:, cols(e)],
                                            ALU.mult).then_inc(side_dve, 1)
                elif kind == "f_stats":
                    dve.wait_ge(side_dve, upto("side_dve", ("f", e[1], e[2])))
                    norm_stats(tiles(ff[:, cols(e)]), count(e), e)

            walk(dve, do)

        @block.gpsimd
        def _(pool):
            nc.gpsimd.memset(minus_half[:, :], -0.5)
            nc.gpsimd.memset(qs[:, :, :, :, :].bitcast(F32), 0.0).then_inc(q_cleared, 1)

            def do(e):
                kind = e[0]
                if kind == "unit":
                    _, b, g, i = e
                    qh, kt, heads, width = UNITS[i]
                    if kt < 4 * qh or not last_of_set(i):
                        return
                    pool.wait_ge(exp_done, upto("unit", e))
                    d = probs[:, set_of(e) % P_RING, 0:4 * width].rearrange("p (j q) -> p j q", j=4)[:, :, 0:P]
                    nc.gpsimd.affine_select(out=d, in_=d, pattern=[[0, 4], [1, P]], compare_op=ALU.is_ge, fill=0.0,
                                            base=0, channel_multiplier=-1).then_inc(masked, 1)
                elif kind == "q_split" and e[1] > 0 and e[3] in (0, 2, 4):
                    _, b, h, i = e
                    if i == 0:
                        pool.wait_ge(side_dve, upto("side_dve", ("qb", b, h)))
                    else:
                        pool.wait_ge(q_split_steps, upto(kind, e, back=1))
                    split_step(nc.gpsimd, i, *q_split_of(h)).then_inc(q_split_steps, 1)
                elif kind == "k_split" and e[1] > 0 and e[2] in (0, 2, 4):
                    _, b, i = e
                    if i == 0:
                        pool.wait_ge(side_dve, upto("side_dve", ("kb", b)))
                    else:
                        pool.wait_ge(k_split_steps, upto(kind, e, back=1))
                    split_step(nc.gpsimd, i, *k_split_of).then_inc(k_split_steps, 1)
                elif kind == "m_split":
                    _, b, g, h, i = e
                    par = g % 2
                    parts = [m_parts[:, par, h, :].rearrange("p (a n x) -> p a n x", a=2, n=3)[:, :, n, :]
                             for n in range(3)]
                    whole, rest = (m[:, par, h, :].rearrange("p (a x) -> p a x", a=2) for m in (neg_max, neg_rest))
                    if i == 0:
                        pool.wait_ge(side_dve, upto("side_dve", ("max", b, g, MAX_END[h])))
                        if G * b + g >= 2:
                            pool.wait_ge(side_act, upto("side_act", ("mT",) + earlier_group(b, g, 2) + (h,)))
                        nc.gpsimd.tensor_scalar(out=neg_max[:, par, h, :], in0=row_max[:, par, h, :], scalar1=-1.0,
                                                scalar2=None, op0=ALU.mult).then_inc(m_split_steps, 1)
                    else:
                        pool.wait_ge(m_split_steps, upto(kind, e, back=1))
                        split_step(nc.gpsimd, i, None, None, whole, rest, parts).then_inc(m_split_steps, 1)
                elif kind == "vB_copy":
                    b = e[1]
                    pool.wait_ge(side_dve, upto("side_dve", ("v", b, 1)))
                    if b > 0:
                        pool.wait_ge(pv_done, upto("pv", ("pv", b - 1, 3, 1, 7)))
                    nc.gpsimd.tensor_copy(vB[:, :, 0:2 * HD:2], vA[:, :, 0:2 * HD:2]).then_inc(vB_set, 1)
                elif kind.endswith("_rstd"):
                    s, n = plan.n["ln", stats_of(e)] % 2, ln_tiles(e)
                    pool.wait_ge(ln_aggr, upto("ln", stats_of(e)))
                    nc.gpsimd.tensor_scalar(out=var_eps[:, s, 0:n], in0=mv[:, s, 0:n, 1], scalar1=EPS,
                                            scalar2=None, op0=ALU.add).then_inc(ln_eps, 1)
                    to_dve = on_dve((kind[:-5] + "_norm",) + e[1:])
                    if not to_dve:
                        nc.gpsimd.tensor_scalar(out=neg_mean[:, s, 0:n], in0=mv[:, s, 0:n, 0], scalar1=-1.0,
                                                scalar2=None, op0=ALU.mult).then_inc(ln_neg, 1)
                    pool.wait_ge(ln_eps, upto("rstd", e))
                    nc.gpsimd.tensor_tensor(out=rstd[:, s, 0:n], in0=var_eps[:, s, 0:n], in1=minus_half[:, 0:n],
                                            op=ALU.pow).then_inc(ln_rstd, 1)
                    if not to_dve:
                        pool.wait_ge(ln_neg, upto("rstd", e))
                        pool.wait_ge(ln_rstd, upto("rstd", e))
                        nc.gpsimd.tensor_tensor(out=shift_by[:, s, 0:n], in0=neg_mean[:, s, 0:n],
                                                in1=rstd[:, s, 0:n], op=ALU.mult).then_inc(ln_ready, 1)
                elif kind == "x1" and not on_dve(e):
                    pool.wait_ge(normed[0], upto_moved(("y_norm",) + e[1:]))
                    pool.wait_ge(xres_loaded, upto("xres_load", ("xres_load", e[1]), each=16))
                    add_residual(nc.gpsimd, e).then_inc(x1_ready[0], 1)
                elif kind == "diff" and not on_dve(e):
                    pool.wait_ge(side_act, upto("side_act", ("nT",) + e[1:]))
                    token_shift(nc.gpsimd, e).then_inc(shift_ready[0], 1)
                elif kind == "sq" and not on_dve(e):
                    pool.wait_ge(side_act, upto("side_act", ("k",) + e[1:]))
                    square(nc.gpsimd, e).then_inc(k_act_ready[0], 1)
                elif kind == "out" and not on_dve(e):
                    pool.wait_ge(normed[0], upto_moved(("f_norm",) + e[1:]))
                    if e[1] > 0:
                        pool.wait_ge(out_stored[half_of(e[1], e[2])], in_batch(e, 16, 0))
                    add_ffn(nc.gpsimd, e).then_inc(fin_ready[0], 1)

            walk(pool, do)



def rotary_order():
    half = HD // 2
    near = [2 * i for i in range(half)] + [2 * i + 1 for i in range(half)]
    far = [2 * i + 1 for i in range(half)] + [2 * i for i in range(half)]
    return near, far


def constant_array():
    half = HD // 2
    freqs = (np.float32(1.0) / np.float32(THETA) ** (np.arange(0, HD, 2, dtype=np.float32) / np.float32(HD)))
    ang = np.arange(S, dtype=np.float32)[:, None] * freqs.astype(np.float32)[None, :]
    cos, sin = np.cos(ang).astype(np.float32), np.sin(ang).astype(np.float32)
    cos8 = np.concatenate([cos, cos], axis=1).T
    sin8 = np.concatenate([-sin, sin], axis=1).T
    c = np.zeros((P, C_COLS), np.float32)
    c[:, C_ID:C_ID + P] = np.eye(P, dtype=np.float32)
    c[:, C_MASK + S - P:C_MASK + S] = np.where(np.arange(P)[None, :] > np.arange(P)[:, None], NEG, 0.0)
    for h in range(2):
        c[32 * h:32 * h + HD, C_KCOS:C_KCOS + HALF] = cos8[:, h * HALF:(h + 1) * HALF]
        c[32 * h:32 * h + HD, C_KSIN:C_KSIN + HALF] = sin8[:, h * HALF:(h + 1) * HALF]
    c[:, C_COS:C_COS + S] = np.tile(np.repeat(cos8, 2, axis=0), (P // (2 * HD), 1))
    c[:, C_SIN:C_SIN + S] = np.tile(np.repeat(sin8, 2, axis=0), (P // (2 * HD), 1))
    return c


def weight_array(wq, wk, wv, wo, w_r, w_k, w_v, mu_r, mu_k):
    near, far = rotary_order()
    w = np.zeros((P, W_COLS), np.float32)
    for col, order in ((W_QA, near), (W_QB, far)):
        rows = [HD * (4 * g + 2 * r + a) + d for a in range(2) for g in range(G) for d in order for r in range(2)]
        w[:, col:col + P] = wq[rows, :].T
    w[:, W_KA:W_KA + HD] = wk[:, near]
    w[:, W_KB:W_KB + HD] = wk[:, far]
    w[:, W_V:W_V + HD] = wv
    w[:, W_O:W_O + D] = wo.T
    w[:, W_R:W_R + D] = w_r.T
    w[:, W_K:W_K + D] = w_k.T
    w[:, W_VF:W_VF + D] = w_v.T
    w[:, W_MU] = mu_r
    w[:, W_MU + 1] = mu_k
    return w


def kernel(L0_attn_x, L0_attn_wq, L0_attn_wk, L0_attn_wv, L0_attn_wo, L0_ffn_W_r, L0_ffn_W_k,
           L0_ffn_W_v, L0_ffn_mu_r, L0_ffn_mu_k):
    import concourse.bacc as bacc
    from concourse.bass_utils import run_bass_kernel_spmd

    a = np.asarray
    arrays = {
        "x": np.ascontiguousarray(a(L0_attn_x)),
        "weights": weight_array(a(L0_attn_wq), a(L0_attn_wk), a(L0_attn_wv), a(L0_attn_wo), a(L0_ffn_W_r),
                                a(L0_ffn_W_k), a(L0_ffn_W_v), a(L0_ffn_mu_r), a(L0_ffn_mu_k)),
        "consts": constant_array(),
    }
    nc = bacc.Bacc("TRN2", target_bir_lowering=False, num_devices=1)
    ins = {n: nc.dram_tensor(n, v.shape, F32, kind="ExternalInput").ap() for n, v in arrays.items()}
    out = nc.dram_tensor("out", (B, S, D), F32, kind="ExternalOutput").ap()
    q_dram = nc.dram_tensor("q_rows_dram", (2, len(Q_PART), P, HALF), BF16, kind="Internal").ap()
    k_dram = nc.dram_tensor("k_parts_dram", (3, HD, S), BF16, kind="Internal").ap()
    layer(nc, ins["x"], ins["weights"], ins["consts"], out, q_dram, k_dram)
    result = run_bass_kernel_spmd(nc, [arrays], core_ids=[0])
    return result.results[0]["out"]
```
